# Optimizing a Trainium2 kernel written in Bass

```python
import numpy as np
import jax
import jax.numpy as jnp

def _softmax(x, axis=-1):
    return jax.nn.softmax(x, axis=axis)

def _gelu(x):
    return jax.nn.gelu(x, approximate=True)

def _silu(x):
    return jax.nn.silu(x)

def _sigmoid(x):
    return jax.nn.sigmoid(x)

def _layernorm(x, axis=-1, eps=1e-05):
    m = jnp.mean(x, axis=axis, keepdims=True)
    v = jnp.var(x, axis=axis, keepdims=True)
    return (x - m) / jnp.sqrt(v + eps)

def _scatter_add(tgt, idx, src, axis=0):
    return tgt.at[idx].add(src)

def _segment_sum(src, seg, n):
    return jax.ops.segment_sum(src, seg, n)
kernel_name = 'mk_adj_resnorm_d1_adj_r2_269e8a'

def setup_inputs(seed: int=0):
    np.random.seed(seed)
    _w = jnp.asarray

    def _rec_inputs():
        import jax
        import jax.numpy as jnp
        _gk = jax.random.key(seed)
        x = -9.806e-05 + 1 * jax.random.normal(jax.random.fold_in(_gk, 1), (8192, 128), jnp.float32)
        _a = jax.random.bernoulli(jax.random.fold_in(_gk, 2), 0.000976562, (8192, 8192))
        _a = jnp.logical_or(_a, jnp.swapaxes(_a, -1, -2))
        _a = jnp.logical_or(_a, jnp.eye(8192, dtype=bool))
        _af = _a.astype(jnp.float32)
        adj = _af
        return (x, adj)
    x, adj = _rec_inputs()

    def _L0_gnn_setup():
        import jax, jax.numpy as jnp
        import numpy as np
        N, F_IN, HEADS, F_OUT = (2048, 128, 4, 32)
        DENSITY = 0.05
        key = jax.random.key(seed)
        k_x, k_adj, k_w, k_as, k_ad, k_b = jax.random.split(key, 6)
        x = jax.random.normal(k_x, (N, F_IN), dtype=jnp.float32)
        adj = (jax.random.uniform(k_adj, (N, N)) < DENSITY).astype(jnp.float32)
        adj = jnp.maximum(adj, jnp.eye(N, dtype=jnp.float32))
        weight = jax.random.normal(k_w, (HEADS * F_OUT, F_IN), dtype=jnp.float32) * 0.1
        att_src = jax.random.normal(k_as, (1, HEADS, F_OUT), dtype=jnp.float32) * 0.1
        att_dst = jax.random.normal(k_ad, (1, HEADS, F_OUT), dtype=jnp.float32) * 0.1
        bias = jax.random.normal(k_b, (HEADS * F_OUT,), dtype=jnp.float32) * 0.1
        return {'x': x, 'adj_matrix': adj, 'weight': weight, 'att_src': att_src, 'att_dst': att_dst, 'bias': bias}
    _L0_gnn_all = _L0_gnn_setup()
    _L0_gnn_in = {k: v for k, v in _L0_gnn_all.items() if k in ('weight', 'att_src', 'att_dst', 'bias')}
    del _L0_gnn_all
    return {'x': x, 'adj': adj, 'L0_gnn_weight': _L0_gnn_in['weight'], 'L0_gnn_att_src': _L0_gnn_in['att_src'], 'L0_gnn_att_dst': _L0_gnn_in['att_dst'], 'L0_gnn_bias': _L0_gnn_in['bias']}

def reference(x, adj, L0_gnn_weight, L0_gnn_att_src, L0_gnn_att_dst, L0_gnn_bias):
    import jax
    import jax.numpy as jnp

    def _L0_gnn_ref(x, adj_matrix, weight, att_src, att_dst, bias):
        import jax, jax.numpy as jnp
        import numpy as np
        N, F_IN, HEADS, F_OUT = (2048, 128, 4, 32)
        DENSITY = 0.05
        n = x.shape[0]
        heads = att_src.shape[1]
        f_out = weight.shape[0] // heads
        h_prime = (x @ weight.T).reshape(n, heads, f_out)
        alpha_src = jnp.sum(h_prime * att_src, axis=-1)
        alpha_dst = jnp.sum(h_prime * att_dst, axis=-1)
        C = alpha_src[None, :, :] + alpha_dst[:, None, :]
        adj_t = adj_matrix.T[..., None]
        tau = adj_t * jnp.exp(jnp.maximum(0.2 * C, C))
        tau_sum = jnp.sum(tau, axis=1, keepdims=True)
        att_weights = tau / tau_sum
        z = jnp.einsum('mnh,nhf->mhf', adj_t * att_weights, h_prime)
        return z.reshape(n, heads * f_out) + bias
    x = _layernorm(x + _L0_gnn_ref(x, adj, L0_gnn_weight, L0_gnn_att_src, L0_gnn_att_dst, L0_gnn_bias), axis=-1)
    return x

_drawn_inputs = setup_inputs


def setup_inputs(seed=0):
    import zlib

    import numpy as np

    out = dict(_drawn_inputs(seed))
    spreads = {}
    factors = {}
    for name, (base, spread) in spreads.items():
        noise = np.random.default_rng([zlib.crc32(name.encode()), seed]).standard_normal(out[name].shape)
        drawn = base * np.exp(spread * noise) if base else spread * noise
        out[name] = jnp.asarray(drawn.astype(out[name].dtype))
    for name, factor in factors.items():
        out[name] = (out[name] * factor).astype(out[name].dtype)
    return out
```

```python
from contextlib import ExitStack

import concourse.bass as bass
from concourse import mybir

P = 128
F32 = mybir.dt.float32
FP16 = mybir.dt.float16
FP8 = mybir.dt.float8e4
U16 = mybir.dt.uint16
ALU = mybir.AluOpType
ACT = mybir.ActivationFunctionType
AX_X = mybir.AxisListType.X

EPS = 1e-5
SLOPE = 0.2
LO = 2.0 ** 11
HI_SCALE = 2.0 ** 8
STEEP = 2.0 ** 64


def gat_kernel(nc, x, xT, adj, weight, weightT, att_src, att_dst, bias, out):
    N, F = x.shape
    H, FO = att_src.shape[1], att_src.shape[2]
    assert F == P and H * FO == P and H == 4

    NT = N // P
    G = 4
    NG = NT // G
    MB = 4
    MC = MB * P
    NCH = N // MC
    W = FO + 1
    VA = 4 * W
    VQ = 2 * W
    RING = 4
    SPLIT = 2
    XB = 8
    NXB = NT // XB
    NQ = 4
    QT = NT // NQ
    assert QT * H * W == MB * H * VA

    scratch = nc.dram_tensor("dst_scores_dram", (NT, H, P), F32, kind="Internal").ap()

    with ExitStack() as ctx:
        def sb(name, shape, dt):
            return ctx.enter_context(nc.sbuf_tensor(name, shape, dt))

        def sem(name):
            return ctx.enter_context(nc.semaphore(name))

        passed = {name: sem(f"passed_{name}") for name in ("act", "dve", "pe")}

        psum = ctx.enter_context(nc.psum_tensor("psum", [P, 2 * MB, 512], F32))

        vals_am = sb("vals_am", [P, NT, H, VA], FP16)
        vals_a = sb("vals_a", [P, NT, H, VQ], FP16)
        masks_raw = sb("masks_raw", [P, RING * H * G * MC // 4], F32)
        masks = masks_raw[:].bitcast(FP8).rearrange("p (r h t m) -> p r h t m", r=RING, h=H, t=G)
        masks16 = masks_raw[:].bitcast(U16).rearrange("p (r h x) -> p r h x", r=RING, h=H)
        feat = masks_raw[:].rearrange("p (t h f) -> p t h f", t=NT, h=H)
        adj8 = sb("adj8", [P, RING, G, MC], FP8)
        adj16 = adj8[:].rearrange("p r t m -> p r (t m)").bitcast(U16)
        drow = sb("drow", [P, 2, MB, H, P], F32)
        xt_sb = sb("xt_sb", [P, 2, XB * P], F32)
        x_res = sb("x_res", [P, 2, MB, F], F32)
        stage_raw = sb("stage_raw", [P, MB * H * VA], F32)
        parts = stage_raw[:].rearrange("p (g s k w) -> p g s k w", g=MB * H, s=2, k=2)
        q_tmp = sb("q_tmp", [P, QT * H * W], F32)
        comb = q_tmp[:, 0:MB * H * VA // 2]
        tot = q_tmp[:, MB * H * VA // 2:MB * H * (VA // 2 + W)].rearrange(
            "p (x w) -> p x w", w=W)
        y = sb("y", [P, MB, F], F32)
        y_out = sb("y_out", [P, MB, F], F32)
        w_nat = sb("w_nat", [P, F], F32)
        w_ext = sb("w_ext", [P, F + 2 * H], F32)
        att_diag = sb("att_diag", [P, 2 * H], F32)
        bias_b = sb("bias_b", [P, F], F32)
        ident = sb("ident", [P, P], F32)
        s_col = sb("s_col", [P, NT, H], F32)
        d_col = sb("d_col", [P, NT, H], F32)
        d_tr = sb("d_tr", [P, 2, P], F32)
        s_max1 = sb("s_max1", [P, H], F32)
        s_max = sb("s_max", [P, H], F32)
        s_neg = sb("s_neg", [P, NT, H], F32)
        s_steep = sb("s_steep", [P, NT, H], F32)
        s_shift = sb("s_shift", [P, NT, H], F32)
        d_shift = sb("d_shift", [P, NT, H], F32)
        p_exp = sb("p_exp", [P, NT, H], F32)
        q_exp = sb("q_exp", [P, NT, H], F32)
        ab_arg = sb("ab_arg", [P, NT, H, 2], F32)
        ab = sb("ab", [P, NT, H, 2], F32)
        den_inv = sb("den_inv", [P, MB * H, 1], F32)
        bn = sb("bn", [P, MB, 6], F32)
        mv = sb("mv", [P, MB, 2], F32)
        rstd = sb("rstd", [P, MB, 1], F32)
        half = sb("half", [P, MB, 1], F32)

        params_loaded = sem("params_loaded")
        att_zeroed = sem("att_zeroed")
        att_loaded = sem("att_loaded")
        xt_loaded = [sem(f"xt_loaded{i}") for i in range(2)]
        ident_zeroed = sem("ident_zeroed")
        ident_ready = sem("ident_ready")
        att_proj = sem("att_proj")
        w_ext_ready = sem("w_ext_ready")
        projected = sem("projected")
        feat_copied = sem("feat_copied")
        scores_copied = sem("scores_copied")
        d_transposed = sem("d_transposed")
        d_tr_ready = sem("d_tr_ready")
        d_stored = sem("d_stored")
        dve_step = sem("dve_step")
        max1_ready = sem("max1_ready")
        max_ready = sem("max_ready")
        exp_args = sem("exp_args")
        exps_ready = sem("exps_ready")
        products = sem("products")
        his_ready = sem("his_ready")
        los_ready = sem("los_ready")
        vals_ready = sem("vals_ready")
        drow_loaded = [sem(f"drow_loaded{i}") for i in range(2)]
        xres_loaded = [sem(f"xres_loaded{i}") for i in range(2)]
        adj_loaded = [sem(f"adj_loaded{i}") for i in range(RING)]
        slot_free = sem("slot_free")
        act_masks = sem("act_masks")
        dve_masks = sem("dve_masks")
        masks_ready = sem("masks_ready")
        block_done = sem("block_done")
        block_free = sem("block_free")
        pool_step = sem("pool_step")
        den_ready = sem("den_ready")
        den_inverted = sem("den_inverted")
        y_ready = sem("y_ready")
        bn_done = sem("bn_done")
        mv_ready = sem("mv_ready")
        out_ready = sem("out_ready")
        out_stored = sem("out_stored")

        xT_b = xT.rearrange("f (b n) -> b f n", b=NXB)
        adj_g = adj.rearrange("(g t p) m -> g p t m", g=NG, t=G)
        x_c = x.rearrange("(c j p) f -> c p j f", c=NCH, j=MB)
        out_c = out.rearrange("(c j p) f -> c p j f", c=NCH, j=MB)
        drow_c = scratch.rearrange("(c j) h p -> c (j h p)", c=NCH)

        block = ctx.enter_context(nc.Block())

        @block.sync
        def _(sp):
            sp.dma_start(w_nat[:], weight).then_inc(params_loaded, 16)
            sp.dma_start(w_ext[:, 0:F], weightT).then_inc(params_loaded, 16)
            sp.dma_start(bias_b[:], bias.rearrange("(a f) -> a f", a=1).to_broadcast([P, F])).then_inc(
                params_loaded, 16)
            sp.wait_ge(att_zeroed, 1)
            for k, att in enumerate((att_src, att_dst)):
                for h in range(H):
                    sp.dma_start(att_diag[h * FO:(h + 1) * FO, k * H + h:k * H + h + 1],
                                 att[0, h, :].rearrange("(f a) -> f a", a=1)).then_inc(att_loaded, 16)
            for b in range(NXB):
                if b >= 2:
                    sp.wait_ge(projected, b - 1)
                sp.dma_start(xt_sb[:, b % 2, :], xT_b[b]).then_inc(xt_loaded[b % 2], 16)
            sp.wait_ge(d_tr_ready, 1)
            sp.dma_start(scratch.rearrange("(k t) h p -> (t h) k p", k=2), d_tr[:]).then_inc(d_stored, 16)
            sp.wait_ge(d_stored, 16)

            def load_scores(c, k):
                sp.dma_start(drow[:, k].rearrange("p j h m -> p (j h m)"),
                             drow_c[bass.ds(c, 1), :].to_broadcast([P, MB * H * P])).then_inc(drow_loaded[k], 16)

            def load_x(c, k):
                sp.dma_start(x_res[:, k], x_c[bass.ds(c, 1)].rearrange("a p j f -> p (a j) f")).then_inc(
                    xres_loaded[k], 16)

            def store_chunk(c):
                sp.wait_ge(out_ready, c + 1)
                sp.dma_start(out_c[bass.ds(c, 1)].rearrange("a p j f -> p (a j) f"), y_out[:]).then_inc(
                    out_stored, 16)

            for k in range(2):
                load_scores(k, k)
                load_x(k, k)
            with sp.Fori(0, NCH // 2 - 1) as i:
                for k in range(2):
                    sp.wait_ge(act_masks, NG * (2 * i + k + 1))
                    sp.wait_ge(dve_masks, NG * (2 * i + k + 1))
                    load_scores(2 * i + k + 2, k)
                    store_chunk(2 * i + k)
                    load_x(2 * i + k + 2, k)
            store_chunk(NCH - 2)
            store_chunk(NCH - 1)
            sp.wait_ge(out_stored, 16 * NCH)

        @block.gpsimd
        def _(pool):
            nc.gpsimd.memset(ident[:], 0.0).then_inc(ident_zeroed, 1)
            pool.wait_ge(ident_zeroed, 1)
            nc.gpsimd.affine_select(out=ident[:], in_=ident[:], compare_op=ALU.not_equal, fill=1.0, base=0,
                                    pattern=[[-1, P]], channel_multiplier=1).then_inc(ident_ready, 1)
            nc.gpsimd.memset(half[:], -0.5).then_inc(pool_step, 1)

            def load_adj(c, g):
                pool.wait_ge(slot_free, NG * c + g + 1)
                pool.dma_start(adj8[:, g % RING],
                               adj_g[g][:, :, c * MC:(c + 1) * MC]).then_inc(adj_loaded[g % RING], 16)

            def bank_pairs(ap):
                return ap.rearrange("p g s k w -> p (g s) k w")

            STEPS = 7

            def combine(c):
                n = 1 + STEPS * c
                pool.wait_ge(block_free, MB * (c + 2))
                pv = bank_pairs(parts)
                cv = comb.rearrange("p (x w) -> p x w", w=W)
                nc.gpsimd.tensor_scalar(pv[:, :, 1, :], pv[:, :, 1, :], 1.0 / LO, None, ALU.mult).then_inc(pool_step, 1)
                pool.wait_ge(pool_step, n + 1)
                nc.gpsimd.tensor_tensor(cv, pv[:, :, 0, :], pv[:, :, 1, :], ALU.add).then_inc(pool_step, 1)
                pool.wait_ge(pool_step, n + 2)

            def total(c):
                n = 1 + STEPS * c
                cv = comb.rearrange("p (x w) -> p x w", w=W)
                abv = ab[:, bass.ts(c, MB)].rearrange("p j h s -> p (j h s)").unsqueeze(2)
                nc.gpsimd.tensor_tensor(cv, cv, abv.to_broadcast([P, 2 * MB * H, W]), ALU.mult).then_inc(pool_step, 1)
                pool.wait_ge(pool_step, n + 3)
                c2 = comb.rearrange("p (x s w) -> p x s w", s=2, w=W)
                nc.gpsimd.tensor_tensor(tot, c2[:, :, 0], c2[:, :, 1], ALU.add).then_inc(den_ready, 1)

            def normalise(c):
                n = 6 + STEPS * c
                pool.wait_ge(mv_ready, c + 1)
                nc.gpsimd.tensor_scalar(rstd[:], mv[:, :, 1:2], EPS, None, ALU.add).then_inc(pool_step, 1)
                pool.wait_ge(pool_step, n + 1)
                nc.gpsimd.tensor_tensor(rstd[:], rstd[:], half[:], ALU.pow).then_inc(pool_step, 1)
                pool.wait_ge(pool_step, n + 2)
                if c:
                    pool.wait_ge(out_stored, 16 * c)
                for j in range(MB):
                    last = nc.gpsimd.tensor_scalar(y_out[:, j], y[:, j], mv[:, j, 0:1], rstd[:, j],
                                                   ALU.subtract, ALU.mult)
                last.then_inc(out_ready, 1)

            def residual(c):
                n = 4 + STEPS * c
                k = c % 2
                pool.wait_ge(xres_loaded[k], 16 * (c // 2 + 1))
                xv = x_res[:, k]
                nc.gpsimd.tensor_tensor(xv, xv, bias_b[:].unsqueeze(1).to_broadcast([P, MB, F]), ALU.add).then_inc(
                    pool_step, 1)
                pool.wait_ge(den_inverted, c + 1)
                yv = y[:].rearrange("p j (h f) -> p (j h) f", h=H)
                nc.gpsimd.tensor_tensor(yv, tot[:, :, 0:FO], den_inv[:].to_broadcast([P, MB * H, FO]),
                                        ALU.mult).then_inc(pool_step, 1)
                pool.wait_ge(pool_step, n + 2)
                nc.gpsimd.tensor_tensor(y[:], y[:], xv, ALU.add).then_inc(y_ready, 1)

            def chunk(c):
                for g in range(NG):
                    load_adj(c, g)
                    if c and g == 6:
                        combine(c - 1)
                    if c and g == 7:
                        total(c - 1)
                    if c and g == 8:
                        residual(c - 1)
                    if c and g == 11:
                        normalise(c - 1)

            pool.wait_ge(max1_ready, 1)
            nc.gpsimd.partition_all_reduce(s_max[:], s_max1[:], P, bass.bass_isa.ReduceOp.max).then_inc(max_ready, 1)
            pool.wait_ge(params_loaded, 48)
            for c in range(NCH):
                chunk(c)
            combine(NCH - 1)
            total(NCH - 1)
            residual(NCH - 1)
            normalise(NCH - 1)

        @block.scalar
        def _(act):
            for b in range(NXB):
                act.wait_ge(projected, b + 1)
                src = psum[:, MB * (b % 2):MB * (b % 2 + 1), 0:2 * (F + 2 * H)].rearrange(
                    "p a (t f) -> p a t f", t=2)[:, :, :, 0:F]
                dst = feat[:, b * XB:(b + 1) * XB].rearrange("p (a t) h f -> p a t (h f)", t=2)
                nc.scalar.activation(dst, src, ACT.Copy).then_inc(feat_copied, 1)
            act.wait_ge(exp_args, 1)
            nc.scalar.activation(p_exp[:], s_shift[:], ACT.Exp)
            nc.scalar.activation(q_exp[:], s_shift[:], ACT.Exp, scale=SLOPE)
            nc.scalar.activation(ab[:], ab_arg[:], ACT.Exp).then_inc(exps_ready, 1)
            for q in range(NQ):
                va = vals_am[:, q * QT:(q + 1) * QT].rearrange("p t h w -> p (t h) w")
                vq = vals_a[:, q * QT:(q + 1) * QT].rearrange("p t h w -> p (t h) w")
                pt = stage_raw[:].rearrange("p (x w) -> p x w", w=W)
                qt = q_tmp[:].rearrange("p (x w) -> p x w", w=W)
                act.wait_ge(products, 2 * q + 1)
                nc.scalar.activation(va[:, :, 0:W], pt, ACT.Copy, scale=1.0 / LO).then_inc(his_ready, 1)
                act.wait_ge(products, 2 * q + 2)
                nc.scalar.activation(vq[:, :, 0:W], qt, ACT.Copy, scale=1.0 / LO).then_inc(his_ready, 1)
                nc.scalar.activation(va[:, :, 2 * W:3 * W], qt, ACT.Copy, scale=-1.0 / LO)
                act.wait_ge(los_ready, 2 * q + 2)
                nc.scalar.activation(va[:, :, 3 * W:4 * W], vq[:, :, W:2 * W], ACT.Copy, scale=-1.0).then_inc(
                    vals_ready, 1)
            act.wait_ge(los_ready, 2 * NQ)

            def compare(c, k, g):
                act.wait_ge(slot_free, NG * c + g + 1)
                act.sem_inc(passed["act"], 1)
                for h in range(SPLIT):
                    for t in range(G):
                        n = g * G + t
                        last = nc.scalar.activation(
                            masks[:, g % RING, h, t, :].rearrange("p (j m) -> p j m", j=MB), drow[:, k, :, h, :],
                            ACT.Sigmoid, scale=STEEP, bias=s_steep[:, n, h:h + 1], saturate=False)
                last.then_inc(act_masks, 1)

            def copy_out(c, first=False):
                for j in range(MB):
                    if j < MB - 1:
                        act.wait_ge(block_done, (MB - 1) * c + j + 1)
                    else:
                        act.wait_ge(slot_free, RING + NG * (c + 1))
                    if j == 0 and not first:
                        act.wait_ge(den_ready, c)
                    nc.scalar.activation(
                        stage_raw[:, j * H * VA:(j + 1) * H * VA].rearrange("p (a w) -> p a w", a=2),
                        psum[:, 2 * j:2 * j + 2, 0:2 * VA], ACT.Copy).then_inc(block_free, 1)

            def chunk(c, k, loads, tail):
                act.wait_ge(drow_loaded[k], 16 * loads)
                for g in range(NG):
                    compare(c, k, g)
                    if g == 2 and tail:
                        copy_out(c - 1, first=tail == "first")

            chunk(0, 0, 1, False)
            chunk(1, 1, 1, "first")
            with act.Fori(1, NCH // 2) as i:
                chunk(2 * i, 0, i + 1, True)
                chunk(2 * i + 1, 1, i + 1, True)
            copy_out(NCH - 1)

        @block.vector
        def _(dve):
            steps = [0]

            def link(ins):
                steps[0] += 1
                ins.then_inc(dve_step, 1)
                dve.wait_ge(dve_step, steps[0])

            nc.vector.memset(att_diag[:], 0.0).then_inc(att_zeroed, 1)
            dve.wait_ge(params_loaded, 48)
            dve.wait_ge(att_proj, 1)
            nc.vector.tensor_copy(w_ext[:, F:F + 2 * H], psum[:, 2 * MB - 1, 0:2 * H]).then_inc(w_ext_ready, 1)
            for b in range(NXB):
                dve.wait_ge(feat_copied, b + 1)
                src = psum[:, MB * (b % 2):MB * (b % 2 + 1), 0:2 * (F + 2 * H)].rearrange(
                    "p a (t f) -> p a t f", t=2)
                for k, col in enumerate((s_col, d_col)):
                    dst = col[:, b * XB:(b + 1) * XB].rearrange("p (a t) h -> p a t h", t=2)
                    last = nc.vector.tensor_copy(dst, src[:, :, :, F + k * H:F + (k + 1) * H])
                last.then_inc(scores_copied, 1)
            dve.wait_ge(scores_copied, NXB)
            nc.vector.tensor_reduce(s_max1[:], s_col[:].rearrange("p t h -> p h t"), AX_X, ALU.max).then_inc(
                max1_ready, 1)
            nc.vector.tensor_scalar(s_neg[:], s_col[:], -1.0, None, ALU.mult)
            link(nc.vector.tensor_scalar(s_steep[:], s_col[:], STEEP, None, ALU.mult))
            dve.wait_ge(d_transposed, 1)
            nc.vector.tensor_copy(d_tr[:], psum[:, 0, 0:2 * P].rearrange("p (k m) -> p k m", k=2)).then_inc(
                d_tr_ready, 1)
            dve.wait_ge(max_ready, 1)
            sm = s_max[:].unsqueeze(1).to_broadcast([P, NT, H])
            nc.vector.tensor_tensor(s_shift[:], s_col[:], sm, ALU.subtract)
            link(nc.vector.tensor_tensor(d_shift[:], d_col[:], sm, ALU.add))
            nc.vector.tensor_scalar(ab_arg[:, :, :, 0], d_shift[:], 1.0 - SLOPE, 0.0, ALU.mult, ALU.min)
            nc.vector.tensor_scalar(ab_arg[:, :, :, 1], d_shift[:], SLOPE - 1.0, 0.0, ALU.mult, ALU.min).then_inc(
                exp_args, 1)
            dve.wait_ge(exps_ready, 1)
            nc.vector.tensor_scalar(p_exp[:], p_exp[:], HI_SCALE * LO, None, ALU.mult)
            link(nc.vector.tensor_scalar(q_exp[:], q_exp[:], HI_SCALE * LO, None, ALU.mult))
            dve.wait_ge(feat_copied, NXB)
            for q in range(NQ):
                tiles = slice(q * QT, (q + 1) * QT)
                va = vals_am[:, tiles].rearrange("p t h w -> p (t h) w")
                vq = vals_a[:, tiles].rearrange("p t h w -> p (t h) w")
                hv = feat[:, tiles].rearrange("p t h f -> p (t h) f")
                pt = stage_raw[:].rearrange("p (x w) -> p x w", w=W)
                qt = q_tmp[:].rearrange("p (x w) -> p x w", w=W)
                if q:
                    dve.wait_ge(vals_ready, q)
                    dve.wait_ge(los_ready, 2 * q)
                for tmp, e in ((pt, p_exp), (qt, q_exp)):
                    ev = e[:, tiles].rearrange("p t h -> p (t h)").unsqueeze(2)
                    nc.vector.tensor_tensor(tmp[:, :, 0:FO], hv, ev.to_broadcast([P, QT * H, FO]), ALU.mult)
                    nc.vector.tensor_copy(tmp[:, :, FO:W], ev).then_inc(products, 1)
                for r, (tmp, v) in enumerate(((pt, va), (qt, vq))):
                    dve.wait_ge(his_ready, 2 * q + r + 1)
                    dve.wait_ge(products, 2 * q + r + 1)
                    nc.vector.scalar_tensor_tensor(out=v[:, :, W:2 * W], in0=v[:, :, 0:W], scalar=-LO, in1=tmp,
                                                   op0=ALU.mult, op1=ALU.add).then_inc(los_ready, 1)
            dve.wait_ge(los_ready, 2 * NQ)

            def masks_of(c, k, g):
                r = g % RING
                dve.wait_ge(slot_free, NG * c + g + 1)
                dve.sem_inc(passed["dve"], 1)
                for h in range(SPLIT, H):
                    for t in range(G):
                        n = g * G + t
                        last = nc.vector.tensor_scalar(
                            masks[:, r, h, t, :].rearrange("p (j m) -> p j m", j=MB), drow[:, k, :, h, :],
                            s_neg[:, n, h:h + 1], None, ALU.is_gt, saturate=False)
                last.then_inc(dve_masks, 1)

            def and_adj(c, g, loads):
                r = g % RING
                dve.wait_ge(adj_loaded[r], 16 * loads)
                for lo, hi, done in ((0, SPLIT, act_masks), (SPLIT, H, dve_masks)):
                    dve.wait_ge(done, NG * c + g + 1)
                    m = masks16[:, r, lo:hi]
                    a = adj16[:, r].unsqueeze(1).to_broadcast([P, hi - lo, G * MC // 2])
                    nc.vector.tensor_tensor(m, m, a, ALU.bitwise_and).then_inc(masks_ready, 1)

            def invert(c):
                dve.wait_ge(den_ready, c + 1)
                nc.vector.reciprocal(den_inv[:], tot[:, :, FO:W]).then_inc(den_inverted, 1)

            def stats(c):
                dve.wait_ge(y_ready, c + 1)
                for j in range(MB):
                    last = nc.vector.bn_stats(bn[:, j], y[:, j])
                last.then_inc(bn_done, 1)
                dve.wait_ge(bn_done, c + 1)
                dve.sem_inc(passed["dve"], 1)
                for j in range(MB):
                    last = nc.vector.bn_aggr(mv[:, j], bn[:, j])
                last.then_inc(mv_ready, 1)

            def chunk(c, k, loads, tail):
                dve.wait_ge(drow_loaded[k], 16 * loads)
                for g in range(NG):
                    masks_of(c, k, g)
                    and_adj(c, g, (NG // RING) * c + g // RING + 1)
                    if tail and g == 8:
                        invert(c - 1)
                    if tail and g == 10:
                        stats(c - 1)

            chunk(0, 0, 1, False)
            chunk(1, 1, 1, "first")
            with dve.Fori(1, NCH // 2) as i:
                chunk(2 * i, 0, i + 1, True)
                chunk(2 * i + 1, 1, i + 1, True)
            invert(NCH - 1)
            stats(NCH - 1)

        @block.tensor
        def _(pe):
            pe.sem_inc(slot_free, RING)
            pe.wait_ge(params_loaded, 48)
            pe.wait_ge(att_loaded, 16 * 2 * H)
            nc.tensor.matmul(psum[:, 2 * MB - 1, 0:2 * H], w_nat[:], att_diag[:], start=True, stop=True).then_inc(
                att_proj, 1)
            pe.wait_ge(w_ext_ready, 1)
            for b in range(NXB):
                pe.wait_ge(xt_loaded[b % 2], 16 * (b // 2 + 1))
                if b >= 2:
                    pe.wait_ge(feat_copied, b - 1)
                    pe.wait_ge(scores_copied, b - 1)
                for i in range(XB):
                    o = (i % 2) * (F + 2 * H)
                    last = nc.tensor.matmul(psum[:, MB * (b % 2) + i // 2, o:o + F + 2 * H],
                                            xt_sb[:, b % 2, i * P:(i + 1) * P], w_ext[:], start=True, stop=True,
                                            skip_group_check=True)
                last.then_inc(projected, 1)
            pe.wait_ge(ident_ready, 1)
            pe.wait_ge(feat_copied, NXB)
            pe.wait_ge(scores_copied, NXB)
            for k in range(2):
                last = nc.tensor.matmul(psum[:, 0, k * P:(k + 1) * P],
                                        d_col[:, k * NT // 2:(k + 1) * NT // 2].rearrange("p t h -> p (t h)"),
                                        ident[:], start=True, stop=True, skip_group_check=True)
            last.then_inc(d_transposed, 1)
            pe.wait_ge(d_tr_ready, 1)
            pe.sem_inc(block_free, MB)

            with pe.Fori(0, NCH) as c:
                for g in range(NG):
                    r = g % RING
                    pe.wait_ge(masks_ready, 2 * (NG * c + g + 1))
                    pe.sem_inc(passed["pe"], 1)
                    if g % (NG // NQ) == 0:
                        pe.wait_ge(vals_ready, g // (NG // NQ) + 1)
                    for j in range(MB):
                        if g == 0:
                            pe.wait_ge(block_free, MB * c + j + 1)
                            pe.sem_inc(passed["pe"], 1)
                        js = slice(j * P, (j + 1) * P)
                        for t in range(G):
                            n = g * G + t
                            first, final = n == 0, n == NT - 1
                            for h in range(H):
                                o = (h % 2) * VA
                                nc.tensor.matmul(psum[:, 2 * j + h // 2, o:o + VA], masks[:, r, h, t, js],
                                                 vals_am[:, n, h, :], start=first and h % 2 == 0, stop=False,
                                                 skip_group_check=True)
                            for a in range(2):
                                o = psum[:, 2 * j + a, 0:2 * VA].rearrange("p (h w) -> p h w", h=2)[:, :, VQ:VA]
                                last = nc.tensor.matmul(o, adj8[:, r, t, js], vals_a[:, n, 2 * a:2 * a + 2, :],
                                                        start=False, stop=final, skip_group_check=True)
                        if g == NG - 1 and j < MB - 1:
                            last.then_inc(block_done, 1)
                    last.then_inc(slot_free, 1)

    return nc


_INS = ['x', 'xT', 'adj', 'L0_gnn_weight', 'weightT', 'L0_gnn_att_src', 'L0_gnn_att_dst', 'L0_gnn_bias']


def kernel(**inputs):
    import numpy as _np
    import concourse.bacc as _bacc
    from concourse import mybir as _mybir
    from concourse.bass_utils import run_bass_kernel_spmd as _run

    laid = {k: _np.asarray(v) for k, v in inputs.items()}
    laid['xT'] = laid['x'].T
    laid['weightT'] = laid['L0_gnn_weight'].T
    nc = _bacc.Bacc("TRN2", target_bir_lowering=False, num_devices=1)
    arrays, args = {}, []
    for name in _INS:
        a = _np.ascontiguousarray(laid[name])
        arrays[f"in_{name}_dram"] = a
        args.append(nc.dram_tensor(f"in_{name}_dram", a.shape, _mybir.dt.from_np(a.dtype), kind="ExternalInput").ap())
    out = nc.dram_tensor("out_dram", laid['x'].shape, _mybir.dt.float32, kind="ExternalOutput").ap()
    gat_kernel(nc, *args, out)
    r = _run(nc, [arrays], core_ids=[0])
    return r.results[0]["out_dram"]
```

```python
from contextlib import ExitStack

import concourse.bass as bass
from concourse import mybir

P = 128
F32 = mybir.dt.float32
FP16 = mybir.dt.float16
FP8 = mybir.dt.float8e4
U16 = mybir.dt.uint16
ALU = mybir.AluOpType
ACT = mybir.ActivationFunctionType
AX_X = mybir.AxisListType.X

EPS = 1e-5
SLOPE = 0.2
LO = 2.0 ** 11
HI_SCALE = 2.0 ** 8
STEEP = 2.0 ** 64


def gat_kernel(nc, x, xT, adj, weight, weightT, att_src, att_dst, bias, out):
    N, F = x.shape
    H, FO = att_src.shape[1], att_src.shape[2]
    assert F == P and H * FO == P and H == 4

    NT = N // P
    G = 4
    NG = NT // G
    MB = 4
    MC = MB * P
    NCH = N // MC
    W = FO + 1
    VA = 4 * W
    VQ = 2 * W
    RING = 4
    UNIT = 2
    AU = 4
    UPC = NG // UNIT
    SPLIT = 2
    EXTRA = (1, 3, 6, 9, 12, 14)
    XB = 8
    NXB = NT // XB
    NQ = 8
    QT = NT // NQ
    GPQ = NG // NQ
    assert 2 * QT * H * W == MB * H * VA and GPQ == 2 and UNIT == 2

    scratch = nc.dram_tensor("dst_scores_dram", (NT, H, P), F32, kind="Internal").ap()

    with ExitStack() as ctx:
        def sb(name, shape, dt):
            return ctx.enter_context(nc.sbuf_tensor(name, shape, dt))

        def sem(name):
            return ctx.enter_context(nc.semaphore(name))

        passed = {name: sem(f"passed_{name}") for name in ("act", "dve", "pe")}

        psum = ctx.enter_context(nc.psum_tensor("psum", [P, 2 * MB, 512], F32))

        vals_am_raw = sb("vals_am", [P, NT * H * VA // 2], F32)
        vals_am = vals_am_raw[:].bitcast(FP16).rearrange("p (t h w) -> p t h w", t=NT, h=H)
        xt_sb = vals_am_raw[:, 0:N]
        feat = vals_am_raw[:, NT * H * VA // 4:NT * H * VA // 4 + NT * F].rearrange(
            "p (t h f) -> p t h f", t=NT, h=H)
        vals_a = sb("vals_a", [P, NT, H, VQ], FP16)
        masks_raw = sb("masks_raw", [P, RING * H * G * MC // 4], F32)
        masks = masks_raw[:].bitcast(FP8).rearrange("p (r h t m) -> p r h t m", r=RING, h=H, t=G)
        masks16 = masks_raw[:].bitcast(U16).rearrange("p (r h x) -> p r h x", r=RING, h=H)
        adj8 = sb("adj8", [P, AU, UNIT, G, MC], FP8)
        adj16 = adj8[:].rearrange("p a u t m -> p a u (t m)").bitcast(U16)
        drow = sb("drow", [P, 2, MB, H, P], F32)
        x_res = sb("x_res", [P, 2, MB, F], F32)
        stage_raw = sb("stage_raw", [P, MB * H * VA], F32)
        parts = stage_raw[:].rearrange("p (g s k w) -> p g s k w", g=MB * H, s=2, k=2)
        q_tmp = sb("q_tmp", [P, 2 * QT * H * W], F32)
        comb = q_tmp[:, 0:MB * H * VA // 2]
        tot = q_tmp[:, MB * H * VA // 2:MB * H * (VA // 2 + W)].rearrange(
            "p (x w) -> p x w", w=W)
        y = sb("y", [P, MB, F], F32)
        y_out = sb("y_out", [P, MB, F], F32)
        w_nat = sb("w_nat", [P, F], F32)
        w_ext = sb("w_ext", [P, F + 2 * H], F32)
        att_col = sb("att_col", [P, 2], F32)
        head_rows = sb("head_rows", [P, H], F32)
        att_diag = sb("att_diag", [P, 2, H], F32)
        bias_b = sb("bias_b", [P, F], F32)
        ident = sb("ident", [P, P], F32)
        s_col = sb("s_col", [P, NT, H], F32)
        d_col = sb("d_col", [P, NT, H], F32)
        d_tr = sb("d_tr", [P, 2, P], F32)
        s_max1 = sb("s_max1", [P, H], F32)
        s_max = sb("s_max", [P, H], F32)
        s_neg = sb("s_neg", [P, NT, H], F32)
        s_steep = sb("s_steep", [P, NT, H], F32)
        s_shift = sb("s_shift", [P, NT, H], F32)
        d_shift = sb("d_shift", [P, NT, H], F32)
        p_exp = sb("p_exp", [P, NT, H], F32)
        q_exp = sb("q_exp", [P, NT, H], F32)
        ab_arg = sb("ab_arg", [P, NT, H, 2], F32)
        ab = sb("ab", [P, NT, H, 2, 2], F32)
        den_inv = sb("den_inv", [P, MB * H, 1], F32)
        bn = sb("bn", [P, MB, 6], F32)
        mv = sb("mv", [P, MB, 2], F32)
        rstd = sb("rstd", [P, MB, 1], F32)
        half = sb("half", [P, MB, 1], F32)

        params_loaded = sem("params_loaded")
        att_loaded = sem("att_loaded")
        att_ready = sem("att_ready")
        xt_loaded = [sem(f"xt_loaded{i}") for i in range(NXB)]
        ident_zeroed = sem("ident_zeroed")
        ident_ready = sem("ident_ready")
        bias_loaded = sem("bias_loaded")
        att_proj = sem("att_proj")
        w_ext_ready = sem("w_ext_ready")
        projected = sem("projected")
        feat_copied = sem("feat_copied")
        scores_copied = sem("scores_copied")
        d_transposed = sem("d_transposed")
        d_tr_ready = sem("d_tr_ready")
        d_stored = sem("d_stored")
        dve_step = sem("dve_step")
        max1_ready = sem("max1_ready")
        max_ready = sem("max_ready")
        exp_args = sem("exp_args")
        exps_ready = sem("exps_ready")
        exps_scaled = sem("exps_scaled")
        p_products = sem("p_products")
        q_products = sem("q_products")
        his_ready = sem("his_ready")
        los_ready = sem("los_ready")
        vals_ready = sem("vals_ready")
        drow_loaded = [sem(f"drow_loaded{i}") for i in range(2)]
        xres_loaded = [sem(f"xres_loaded{i}") for i in range(2)]
        adj_loaded = [sem(f"adj_loaded{i}") for i in range(AU)]
        slot_free = sem("slot_free")
        act_masks = sem("act_masks")
        dve_masks = sem("dve_masks")
        masks_ready = sem("masks_ready")
        block_done = sem("block_done")
        block_free = sem("block_free")
        pool_step = sem("pool_step")
        den_ready = sem("den_ready")
        den_inverted = sem("den_inverted")
        y_ready = sem("y_ready")
        var_ready = sem("var_ready")
        rstd_ready = sem("rstd_ready")
        bn_done = sem("bn_done")
        mv_ready = sem("mv_ready")
        out_ready = sem("out_ready")
        out_stored = sem("out_stored")

        xT_b = xT.rearrange("f (b n) -> b f n", b=NXB)
        adj_u = adj.rearrange("(u t p) m -> u p t m", u=UPC, t=UNIT * G)
        x_c = x.rearrange("(c j p) f -> c p j f", c=NCH, j=MB)
        out_c = out.rearrange("(c j p) f -> c p j f", c=NCH, j=MB)
        drow_c = scratch.rearrange("(c j) h p -> c (j h p)", c=NCH)

        def half_of(tmp, q):
            return tmp[:, q % 2 * QT * H * W:(q % 2 + 1) * QT * H * W]

        def part_views(q):
            tiles = slice(q * QT, (q + 1) * QT)
            return (vals_am[:, tiles].rearrange("p t h w -> p (t h) w"),
                    vals_a[:, tiles].rearrange("p t h w -> p (t h) w"),
                    half_of(stage_raw, q).rearrange("p (x w) -> p x w", w=W),
                    half_of(q_tmp, q).rearrange("p (x w) -> p x w", w=W))

        def times_head_factor(engine, tmp, h, e, tiles, done):
            ev = e[:, tiles].rearrange("p t h -> p (t h)").unsqueeze(2)
            tv = tmp.rearrange("p (x w) -> p x w", w=W)
            engine.tensor_tensor(tv[:, :, 0:FO], h[:, tiles].rearrange("p t h f -> p (t h) f"),
                                 ev.to_broadcast([P, QT * H, FO]), ALU.mult).then_inc(done, 1)
            engine.tensor_copy(tv[:, :, FO:W], ev).then_inc(done, 1)

        block = ctx.enter_context(nc.Block())

        @block.sync
        def _(sp):
            for k, att in enumerate((att_src, att_dst)):
                sp.dma_start(att_col[:, k:k + 1], att.rearrange("a h f -> (h f) a")).then_inc(att_loaded, 16)
            sp.dma_start(w_nat[:], weight).then_inc(params_loaded, 16)
            sp.dma_start(w_ext[:, 0:F], weightT).then_inc(params_loaded, 16)
            for b in range(NXB):
                sp.dma_start(xt_sb[:, b * XB * P:(b + 1) * XB * P], xT_b[b]).then_inc(xt_loaded[b], 16)
            sp.dma_start(bias_b[:], bias.rearrange("(a f) -> a f", a=1).to_broadcast([P, F])).then_inc(
                bias_loaded, 16)
            sp.wait_ge(d_tr_ready, 1)
            sp.dma_start(scratch.rearrange("(k t) h p -> (t h) k p", k=2), d_tr[:]).then_inc(d_stored, 16)
            sp.wait_ge(d_stored, 16)

            def load_scores(c, k):
                sp.dma_start(drow[:, k].rearrange("p j h m -> p (j h m)"),
                             drow_c[bass.ds(c, 1), :].to_broadcast([P, MB * H * P])).then_inc(drow_loaded[k], 16)

            def load_x(c, k):
                sp.dma_start(x_res[:, k], x_c[bass.ds(c, 1)].rearrange("a p j f -> p (a j) f")).then_inc(
                    xres_loaded[k], 16)

            def store_chunk(c):
                sp.wait_ge(out_ready, c + 1)
                sp.dma_start(out_c[bass.ds(c, 1)].rearrange("a p j f -> p (a j) f"), y_out[:]).then_inc(
                    out_stored, 16)

            for k in range(2):
                load_scores(k, k)
                load_x(k, k)
            with sp.Fori(0, NCH // 2 - 1) as i:
                for k in range(2):
                    sp.wait_ge(act_masks, NG * (2 * i + k + 1))
                    sp.wait_ge(dve_masks, NG * (2 * i + k + 1))
                    load_scores(2 * i + k + 2, k)
                    store_chunk(2 * i + k)
                    load_x(2 * i + k + 2, k)
            store_chunk(NCH - 2)
            store_chunk(NCH - 1)
            sp.wait_ge(out_stored, 16 * NCH)

        @block.gpsimd
        def _(pool):
            nc.gpsimd.memset(ident[:], 0.0).then_inc(ident_zeroed, 1)
            pool.wait_ge(ident_zeroed, 1)
            nc.gpsimd.affine_select(out=ident[:], in_=ident[:], compare_op=ALU.not_equal, fill=1.0, base=0,
                                    pattern=[[-1, P]], channel_multiplier=1).then_inc(ident_ready, 1)
            nc.gpsimd.memset(half[:], -0.5).then_inc(pool_step, 1)
            pool.wait_ge(pool_step, 1)

            def load_adj(u):
                if u >= AU:
                    pool.wait_ge(slot_free, RING + UNIT * (u - AU + 1))
                pool.dma_start(adj8[:, u % AU].rearrange("p u t m -> p (u t) m"),
                               adj_u[u % UPC][:, :, (u // UPC) * MC:(u // UPC + 1) * MC]).then_inc(
                                   adj_loaded[u % AU], 16)

            STEPS = 6

            def combine(c):
                n = 1 + STEPS * c
                pool.wait_ge(block_free, MB * (c + 2))
                sums = stage_raw[:].rearrange("p (x w) -> p x w", w=W)
                abv = ab[:, c * MB:(c + 1) * MB].rearrange("p j h s k -> p (j h s k)").unsqueeze(2)
                nc.gpsimd.tensor_tensor(sums, sums, abv.to_broadcast([P, 4 * MB * H, W]), ALU.mult).then_inc(
                    pool_step, 1)
                pool.wait_ge(pool_step, n + 1)
                hl = stage_raw[:].rearrange("p (x k w) -> p x k w", k=2, w=W)
                nc.gpsimd.tensor_tensor(comb.rearrange("p (x w) -> p x w", w=W), hl[:, :, 0], hl[:, :, 1],
                                        ALU.add).then_inc(pool_step, 1)
                pool.wait_ge(pool_step, n + 2)

            def total(c):
                c2 = comb.rearrange("p (x s w) -> p x s w", s=2, w=W)
                nc.gpsimd.tensor_tensor(tot, c2[:, :, 0], c2[:, :, 1], ALU.add).then_inc(den_ready, 1)

            def residual(c):
                n = 3 + STEPS * c
                k = c % 2
                pool.wait_ge(xres_loaded[k], 16 * (c // 2 + 1))
                xv = x_res[:, k]
                nc.gpsimd.tensor_tensor(xv, xv, bias_b[:].unsqueeze(1).to_broadcast([P, MB, F]), ALU.add).then_inc(
                    pool_step, 1)
                pool.wait_ge(den_inverted, c + 1)
                yv = y[:].rearrange("p j (h f) -> p (j h) f", h=H)
                nc.gpsimd.tensor_tensor(yv, tot[:, :, 0:FO], den_inv[:].to_broadcast([P, MB * H, FO]),
                                        ALU.mult).then_inc(pool_step, 1)
                pool.wait_ge(pool_step, n + 2)
                nc.gpsimd.tensor_tensor(y[:], y[:], xv, ALU.add).then_inc(y_ready, 1)

            def inverse_std(c, n):
                pool.wait_ge(mv_ready, c + 1)
                nc.gpsimd.tensor_scalar(rstd[:], mv[:, :, 1:2], EPS, None, ALU.add).then_inc(pool_step, 1)
                pool.wait_ge(pool_step, n + 1)
                nc.gpsimd.tensor_tensor(rstd[:], rstd[:], half[:], ALU.pow).then_inc(rstd_ready, 1)

            def normalise(c):
                n = 6 + STEPS * c
                inverse_std(c, n - 1)
                nc.gpsimd.tensor_tensor(y[:], y[:], mv[:, :, 0:1].to_broadcast([P, MB, F]), ALU.subtract).then_inc(
                    pool_step, 1)
                pool.wait_ge(pool_step, n + 1)
                pool.wait_ge(rstd_ready, c + 1)
                if c:
                    pool.wait_ge(out_stored, 16 * c)
                nc.gpsimd.tensor_tensor(y_out[:], y[:], rstd[:].to_broadcast([P, MB, F]), ALU.mult).then_inc(
                    out_ready, 1)

            def chunk(c):
                for u in range(UPC):
                    if c:
                        load_adj(c * UPC + u)
                    if c and u == 3:
                        combine(c - 1)
                        total(c - 1)
                    if c and u == 4:
                        residual(c - 1)
                    if c and u == 6:
                        normalise(c - 1)

            for u in range(AU):
                load_adj(u)
            pool.wait_ge(max1_ready, 1)
            nc.gpsimd.partition_all_reduce(s_max[:], s_max1[:], P, bass.bass_isa.ReduceOp.max).then_inc(max_ready, 1)
            pool.wait_ge(exps_scaled, 1)
            for q in range(NQ):
                if q >= 2:
                    pool.wait_ge(his_ready, 2 * (q - 1))
                    pool.wait_ge(los_ready, 2 * (q - 1))
                if q >= AU:
                    load_adj(q)
                times_head_factor(nc.gpsimd, half_of(q_tmp, q), feat, q_exp, slice(q * QT, (q + 1) * QT), q_products)
            pool.wait_ge(bias_loaded, 16)
            for c in range(NCH):
                chunk(c)
            inverse_std(NCH - 1, 1 + STEPS * (NCH - 1))

        @block.scalar
        def _(act):
            def copy_features(batches):
                for b in batches:
                    act.wait_ge(projected, b + 1)
                    src = psum[:, MB * (b % 2):MB * (b % 2 + 1), 0:2 * (F + 2 * H)].rearrange(
                        "p a (t f) -> p a t f", t=2)[:, :, :, 0:F]
                    dst = feat[:, b * XB:(b + 1) * XB].rearrange("p (a t) h f -> p a t (h f)", t=2)
                    nc.scalar.activation(dst, src, ACT.Copy).then_inc(feat_copied, 1)

            def exponentials():
                act.wait_ge(exp_args, 1)
                nc.scalar.activation(p_exp[:], s_shift[:], ACT.Exp)
                nc.scalar.activation(q_exp[:], s_shift[:], ACT.Exp, scale=SLOPE)
                nc.scalar.activation(ab[:, :, :, :, 0], ab_arg[:], ACT.Exp).then_inc(exps_ready, 1)

            def high_parts(q):
                va, vq, pt, qt = part_views(q)
                act.wait_ge(p_products, 2 * (q + 1))
                act.wait_ge(q_products, 2 * (q + 1))
                nc.scalar.activation(va[:, :, 0:W], pt, ACT.Copy, scale=1.0 / LO).then_inc(his_ready, 1)
                nc.scalar.activation(vq[:, :, 0:W], qt, ACT.Copy, scale=1.0 / LO).then_inc(his_ready, 1)

            def compare(c, k, g):
                act.wait_ge(slot_free, NG * c + g + 1)
                act.sem_inc(passed["act"], 1)
                heads = [(h, t) for h in range(SPLIT) for t in range(G)] + [(SPLIT, 0)] * (g in EXTRA)
                for h, t in heads:
                    n = g * G + t
                    last = nc.scalar.activation(
                        masks[:, g % RING, h, t, :].rearrange("p (j m) -> p j m", j=MB), drow[:, k, :, h, :],
                        ACT.Sigmoid, scale=STEEP, bias=s_steep[:, n, h:h + 1], saturate=False)
                last.then_inc(act_masks, 1)

            def copy_out(c, first=False):
                for j in range(MB):
                    if j < MB - 1:
                        act.wait_ge(block_done, (MB - 1) * c + j + 1)
                    else:
                        act.wait_ge(slot_free, RING + NG * (c + 1))
                    if j == 0 and not first:
                        act.wait_ge(den_ready, c)
                    nc.scalar.activation(
                        stage_raw[:, j * H * VA:(j + 1) * H * VA].rearrange("p (a w) -> p a w", a=2),
                        psum[:, 2 * j:2 * j + 2, 0:2 * VA], ACT.Copy).then_inc(block_free, 1)

            def chunk(c, k, loads, tail):
                act.wait_ge(drow_loaded[k], 16 * loads)
                for g in range(NG):
                    compare(c, k, g)
                    if g == 2 and tail:
                        copy_out(c - 1, first=tail == "first")

            copy_features(range(NXB))
            exponentials()
            high_parts(0)
            act.wait_ge(drow_loaded[0], 16)
            for g in range(NG):
                compare(0, 0, g)
                if g % GPQ == 0 and g + GPQ < NG:
                    high_parts(g // GPQ + 1)
            chunk(1, 1, 1, "first")
            with act.Fori(1, NCH // 2) as i:
                chunk(2 * i, 0, i + 1, True)
                chunk(2 * i + 1, 1, i + 1, True)
            copy_out(NCH - 1)

        @block.vector
        def _(dve):
            steps = [0]

            def link(ins):
                steps[0] += 1
                ins.then_inc(dve_step, 1)
                dve.wait_ge(dve_step, steps[0])

            link(nc.vector.memset(head_rows[:], 0.0))
            for h in range(H):
                link(nc.vector.memset(head_rows[h * FO:(h + 1) * FO, h:h + 1], 1.0))
            dve.wait_ge(att_loaded, 32)
            nc.vector.tensor_tensor(att_diag[:], att_col[:].unsqueeze(2).to_broadcast([P, 2, H]),
                                    head_rows[:].unsqueeze(1).to_broadcast([P, 2, H]), ALU.mult).then_inc(
                                        att_ready, 1)
            dve.wait_ge(params_loaded, 32)
            dve.wait_ge(att_proj, 1)
            nc.vector.tensor_copy(w_ext[:, F:F + 2 * H], psum[:, 6, 0:2 * H]).then_inc(w_ext_ready, 1)
            for b in range(NXB):
                dve.wait_ge(feat_copied, b + 1)
                src = psum[:, MB * (b % 2):MB * (b % 2 + 1), 0:2 * (F + 2 * H)].rearrange(
                    "p a (t f) -> p a t f", t=2)
                for k, col in enumerate((s_col, d_col)):
                    dst = col[:, b * XB:(b + 1) * XB].rearrange("p (a t) h -> p a t h", t=2)
                    last = nc.vector.tensor_copy(dst, src[:, :, :, F + k * H:F + (k + 1) * H])
                last.then_inc(scores_copied, 1)
            dve.wait_ge(scores_copied, NXB)
            nc.vector.tensor_reduce(s_max1[:], s_col[:].rearrange("p t h -> p h t"), AX_X, ALU.max).then_inc(
                max1_ready, 1)
            nc.vector.tensor_scalar(s_neg[:], s_col[:], -1.0, None, ALU.mult)
            link(nc.vector.tensor_scalar(s_steep[:], s_col[:], STEEP, None, ALU.mult))
            dve.wait_ge(d_transposed, 1)
            nc.vector.tensor_copy(d_tr[:], psum[:, 0, 0:2 * P].rearrange("p (k m) -> p k m", k=2)).then_inc(
                d_tr_ready, 1)
            dve.wait_ge(max_ready, 1)
            sm = s_max[:].unsqueeze(1).to_broadcast([P, NT, H])
            nc.vector.tensor_tensor(s_shift[:], s_col[:], sm, ALU.subtract)
            link(nc.vector.tensor_tensor(d_shift[:], d_col[:], sm, ALU.add))
            nc.vector.tensor_scalar(ab_arg[:, :, :, 0], d_shift[:], 1.0 - SLOPE, 0.0, ALU.mult, ALU.min)
            nc.vector.tensor_scalar(ab_arg[:, :, :, 1], d_shift[:], SLOPE - 1.0, 0.0, ALU.mult, ALU.min).then_inc(
                exp_args, 1)
            dve.wait_ge(exps_ready, 1)
            nc.vector.tensor_scalar(q_exp[:], q_exp[:], HI_SCALE * LO, None, ALU.mult).then_inc(exps_scaled, 1)
            link(nc.vector.tensor_scalar(p_exp[:], p_exp[:], HI_SCALE * LO, None, ALU.mult))
            nc.vector.tensor_scalar(ab[:, :, :, :, 1], ab[:, :, :, :, 0], 1.0 / LO, None, ALU.mult)

            def p_of(q):
                if q >= 2:
                    dve.wait_ge(his_ready, 2 * (q - 1))
                    dve.wait_ge(los_ready, 2 * (q - 1))
                times_head_factor(nc.vector, half_of(stage_raw, q), feat, p_exp, slice(q * QT, (q + 1) * QT), p_products)

            def low_parts(q):
                va, vq, pt, qt = part_views(q)
                for r, (tmp, v, made) in enumerate(((pt, va, p_products), (qt, vq, q_products))):
                    dve.wait_ge(made, 2 * (q + 1))
                    dve.wait_ge(his_ready, 2 * q + r + 1)
                    nc.vector.scalar_tensor_tensor(out=v[:, :, W:2 * W], in0=v[:, :, 0:W], scalar=-LO, in1=tmp,
                                                   op0=ALU.mult, op1=ALU.add).then_inc(los_ready, 1)
                dve.wait_ge(los_ready, 2 * (q + 1))
                nc.vector.tensor_scalar(va[:, :, VQ:VA], vq, -1.0, None, ALU.mult).then_inc(vals_ready, 1)

            def masks_of(c, k, g):
                r = g % RING
                dve.wait_ge(slot_free, NG * c + g + 1)
                dve.sem_inc(passed["dve"], 1)
                for h in range(SPLIT, H):
                    for t in range(int(h == SPLIT and g in EXTRA), G):
                        n = g * G + t
                        last = nc.vector.tensor_scalar(
                            masks[:, r, h, t, :].rearrange("p (j m) -> p j m", j=MB), drow[:, k, :, h, :],
                            s_neg[:, n, h:h + 1], None, ALU.is_gt, saturate=False)
                last.then_inc(dve_masks, 1)

            def and_adj(c, g):
                r = g % RING
                u = g // UNIT
                dve.wait_ge(adj_loaded[u % AU], 16 * ((UPC // AU) * c + u // AU + 1))
                for lo, hi, done in ((0, SPLIT, act_masks), (SPLIT, H, dve_masks)):
                    dve.wait_ge(done, NG * c + g + 1)
                    m = masks16[:, r, lo:hi]
                    a = adj16[:, u % AU, g % UNIT].unsqueeze(1).to_broadcast([P, hi - lo, G * MC // 2])
                    nc.vector.tensor_tensor(m, m, a, ALU.bitwise_and).then_inc(masks_ready, 1)

            def invert(c):
                dve.wait_ge(den_ready, c + 1)
                nc.vector.reciprocal(den_inv[:], tot[:, :, FO:W]).then_inc(den_inverted, 1)

            def stats(c):
                dve.wait_ge(y_ready, c + 1)
                for j in range(MB):
                    last = nc.vector.bn_stats(bn[:, j], y[:, j])
                last.then_inc(bn_done, 1)
                dve.wait_ge(bn_done, c + 1)
                dve.sem_inc(passed["dve"], 1)
                for j in range(MB):
                    last = nc.vector.bn_aggr(mv[:, j], bn[:, j])
                last.then_inc(mv_ready, 1)

            def chunk(c, k, loads, tail):
                dve.wait_ge(drow_loaded[k], 16 * loads)
                for g in range(NG):
                    masks_of(c, k, g)
                    and_adj(c, g)
                    if tail and g == 7:
                        invert(c - 1)
                    if tail and g == 9:
                        stats(c - 1)

            p_of(0)
            dve.wait_ge(drow_loaded[0], 16)
            for g in range(NG):
                q = g // GPQ + 1
                if g % GPQ == 0 and q < NQ:
                    p_of(q)
                masks_of(0, 0, g)
                if g == 0:
                    low_parts(0)
                and_adj(0, g)
                if g % GPQ == 1 and q < NQ:
                    low_parts(q)
            chunk(1, 1, 1, True)
            with dve.Fori(1, NCH // 2) as i:
                chunk(2 * i, 0, i + 1, True)
                chunk(2 * i + 1, 1, i + 1, True)

            e = NCH - 1
            last_sums = stage_raw[:].rearrange("p (j x k w) -> p j x k w", j=MB, k=2, w=W)
            cj = q_tmp[:, 0:2 * H * W].rearrange("p (x w) -> p x w", w=W)
            c2 = q_tmp[:, 0:2 * H * W].rearrange("p (x s w) -> p x s w", s=2, w=W)
            tj = tot[:, 0:H]
            dve.wait_ge(xres_loaded[e % 2], 16 * NCH // 2)
            dve.wait_ge(y_ready, e)
            dve.wait_ge(out_stored, 16 * e)
            link(nc.vector.tensor_tensor(x_res[:, e % 2], x_res[:, e % 2],
                                         bias_b[:].unsqueeze(1).to_broadcast([P, MB, F]), ALU.add))
            for j in range(MB):
                dve.wait_ge(block_free, MB * NCH + j + 1)
                abj = ab[:, MB * e + j].rearrange("p h s k -> p (h s) k")[:, :, 0:1]
                link(nc.vector.scalar_tensor_tensor(out=cj, in0=last_sums[:, j, :, 1], scalar=1.0 / LO,
                                                    in1=last_sums[:, j, :, 0], op0=ALU.mult, op1=ALU.add))
                link(nc.vector.tensor_tensor(cj, cj, abj.to_broadcast([P, 2 * H, W]), ALU.mult))
                link(nc.vector.tensor_tensor(tj, c2[:, :, 0], c2[:, :, 1], ALU.add))
                link(nc.vector.reciprocal(den_inv[:, 0:H], tj[:, :, FO:W]))
                link(nc.vector.tensor_tensor(y[:, j].rearrange("p (h f) -> p h f", h=H), tj[:, :, 0:FO],
                                             den_inv[:, 0:H].to_broadcast([P, H, FO]), ALU.mult))
                link(nc.vector.tensor_tensor(y[:, j], y[:, j], x_res[:, e % 2, j], ALU.add))
                link(nc.vector.bn_stats(bn[:, j], y[:, j]))
                last = nc.vector.bn_aggr(mv[:, j], bn[:, j])
            last.then_inc(mv_ready, 1)
            dve.wait_ge(mv_ready, NCH)
            dve.wait_ge(rstd_ready, NCH)
            for j in range(MB):
                last = nc.vector.tensor_scalar(y_out[:, j], y[:, j], mv[:, j, 0:1], rstd[:, j],
                                               ALU.subtract, ALU.mult)
            last.then_inc(out_ready, 1)

        @block.tensor
        def _(pe):
            pe.sem_inc(slot_free, RING)
            pe.wait_ge(params_loaded, 32)
            pe.wait_ge(att_ready, 1)
            nc.tensor.matmul(psum[:, 6, 0:2 * H], w_nat[:], att_diag[:].rearrange("p k h -> p (k h)"), start=True, stop=True).then_inc(
                att_proj, 1)
            pe.wait_ge(w_ext_ready, 1)
            for b in range(NXB):
                pe.wait_ge(xt_loaded[b], 16)
                if b >= 2:
                    pe.wait_ge(feat_copied, b - 1)
                    pe.wait_ge(scores_copied, b - 1)
                for i in range(XB):
                    n = b * XB + i
                    o = (i % 2) * (F + 2 * H)
                    last = nc.tensor.matmul(psum[:, MB * (b % 2) + i // 2, o:o + F + 2 * H],
                                            xt_sb[:, n * P:(n + 1) * P], w_ext[:], start=True, stop=True,
                                            skip_group_check=True)
                last.then_inc(projected, 1)
            pe.wait_ge(ident_ready, 1)
            pe.wait_ge(scores_copied, NXB)
            for k in range(2):
                last = nc.tensor.matmul(psum[:, 0, k * P:(k + 1) * P],
                                        d_col[:, k * NT // 2:(k + 1) * NT // 2].rearrange("p t h -> p (t h)"),
                                        ident[:], start=True, stop=True, skip_group_check=True)
            last.then_inc(d_transposed, 1)
            pe.wait_ge(d_tr_ready, 1)
            pe.sem_inc(block_free, MB)

            with pe.Fori(0, NCH) as c:
                for g in range(NG):
                    r = g % RING
                    pe.wait_ge(masks_ready, 2 * (NG * c + g + 1))
                    pe.sem_inc(passed["pe"], 1)
                    if g % GPQ == 0:
                        pe.wait_ge(vals_ready, g // GPQ + 1)
                    for j in range(MB):
                        if g == 0:
                            pe.wait_ge(block_free, MB * c + j + 1)
                            pe.sem_inc(passed["pe"], 1)
                        js = slice(j * P, (j + 1) * P)
                        for t in range(G):
                            n = g * G + t
                            first, final = n == 0, n == NT - 1
                            for h in range(H):
                                o = (h % 2) * VA
                                nc.tensor.matmul(psum[:, 2 * j + h // 2, o:o + VA], masks[:, r, h, t, js],
                                                 vals_am[:, n, h, :], start=first and h % 2 == 0, stop=False,
                                                 skip_group_check=True)
                            for a in range(2):
                                o = psum[:, 2 * j + a, 0:2 * VA].rearrange("p (h w) -> p h w", h=2)[:, :, VQ:VA]
                                last = nc.tensor.matmul(o, adj8[:, g // UNIT % AU, g % UNIT, t, js], vals_a[:, n, 2 * a:2 * a + 2, :],
                                                        start=False, stop=final, skip_group_check=True)
                        if g == NG - 1 and j < MB - 1:
                            last.then_inc(block_done, 1)
                    last.then_inc(slot_free, 1)

    return nc


_INS = ['x', 'xT', 'adj', 'L0_gnn_weight', 'weightT', 'L0_gnn_att_src', 'L0_gnn_att_dst', 'L0_gnn_bias']


def kernel(**inputs):
    import numpy as _np
    import concourse.bacc as _bacc
    from concourse import mybir as _mybir
    from concourse.bass_utils import run_bass_kernel_spmd as _run

    laid = {k: _np.asarray(v) for k, v in inputs.items()}
    laid['xT'] = laid['x'].T
    laid['weightT'] = laid['L0_gnn_weight'].T
    nc = _bacc.Bacc("TRN2", target_bir_lowering=False, num_devices=1)
    arrays, args = {}, []
    for name in _INS:
        a = _np.ascontiguousarray(laid[name])
        arrays[f"in_{name}_dram"] = a
        args.append(nc.dram_tensor(f"in_{name}_dram", a.shape, _mybir.dt.from_np(a.dtype), kind="ExternalInput").ap())
    out = nc.dram_tensor("out_dram", laid['x'].shape, _mybir.dt.float32, kind="ExternalOutput").ap()
    gat_kernel(nc, *args, out)
    r = _run(nc, [arrays], core_ids=[0])
    return r.results[0]["out_dram"]
```

```python
from contextlib import ExitStack

import concourse.bass as bass
from concourse import mybir

P = 128
F32 = mybir.dt.float32
FP16 = mybir.dt.float16
FP8 = mybir.dt.float8e4
U16 = mybir.dt.uint16
ALU = mybir.AluOpType
ACT = mybir.ActivationFunctionType
AX_X = mybir.AxisListType.X

EPS = 1e-5
SLOPE = 0.2
LO = 2.0 ** 11
HI_SCALE = 2.0 ** 8
STEEP = 2.0 ** 64


def gat_kernel(nc, x, xT, adj, weight, weightT, att_src, att_dst, bias, out):
    N, F = x.shape
    H, FO = att_src.shape[1], att_src.shape[2]
    assert F == P and H * FO == P and H == 4

    NT = N // P
    G = 4
    NG = NT // G
    MB = 4
    MC = MB * P
    NCH = N // MC
    W = FO + 1
    VA = 4 * W
    VQ = 2 * W
    RING = 4
    UNIT = 2
    AU = 4
    UPC = NG // UNIT
    SPLIT = 2
    EXTRA = (4, 6, 8, 10, 12)
    EXTRA_FIRST = (2, 5, 8, 11, 14)
    XB = 8
    NXB = NT // XB
    NQ = 8
    QT = NT // NQ
    GPQ = NG // NQ
    assert 2 * QT * H * W == MB * H * VA and GPQ == 2 and UNIT == 2

    scratch = nc.dram_tensor("dst_scores_dram", (NT, H, P), F32, kind="Internal").ap()

    first_scores = nc.dram_tensor("first_dst_scores_dram", (MB * H, P), F32, kind="Internal").ap()

    with ExitStack() as ctx:
        def sb(name, shape, dt):
            return ctx.enter_context(nc.sbuf_tensor(name, shape, dt))

        def sem(name):
            return ctx.enter_context(nc.semaphore(name))

        passed = {name: sem(f"passed_{name}") for name in ("act", "dve", "pe")}

        psum = ctx.enter_context(nc.psum_tensor("psum", [P, 2 * MB, 512], F32))

        vals_am_raw = sb("vals_am", [P, NT * H * VA // 2], F32)
        vals_am = vals_am_raw[:].bitcast(FP16).rearrange("p (t h w) -> p t h w", t=NT, h=H)
        xt_sb = vals_am_raw[:, 0:N]
        feat = vals_am_raw[:, NT * H * VA // 4:NT * H * VA // 4 + NT * F].rearrange(
            "p (t h f) -> p t h f", t=NT, h=H)
        vals_a = sb("vals_a", [P, NT, H, VQ], FP16)
        masks_raw = sb("masks_raw", [P, RING * H * G * MC // 4], F32)
        masks = masks_raw[:].bitcast(FP8).rearrange("p (r h t m) -> p r h t m", r=RING, h=H, t=G)
        masks16 = masks_raw[:].bitcast(U16).rearrange("p (r h x) -> p r h x", r=RING, h=H)
        adj8 = sb("adj8", [P, AU, UNIT, G, MC], FP8)
        adj16 = adj8[:].rearrange("p a u t m -> p a u (t m)").bitcast(U16)
        drow = sb("drow", [P, 2, MB, H, P], F32)
        x_res = sb("x_res", [P, 2, MB, F], F32)
        stage_raw = sb("stage_raw", [P, MB * H * VA], F32)
        sums = stage_raw[:].rearrange("p (x k w) -> p x k w", k=2, w=W)
        q_tmp = sb("q_tmp", [P, 2 * QT * H * W], F32)
        comb = q_tmp[:, 0:MB * H * 2 * W].rearrange("p (x w) -> p x w", w=W)
        tot = q_tmp[:, MB * H * 2 * W:MB * H * 3 * W].rearrange(
            "p (x w) -> p x w", w=W)
        y_raw = sb("y", [P, QT * H * W], F32)
        hi_tmp = y_raw[:].rearrange("p (x w) -> p x w", w=W)
        y = y_raw[:, 0:MB * F].rearrange("p (j f) -> p j f", j=MB)
        y_out = y_raw[:, MB * F:2 * MB * F].rearrange("p (j f) -> p j f", j=MB)
        w_nat = sb("w_nat", [P, F], F32)
        w_ext = sb("w_ext", [P, F + 2 * H], F32)
        att_col = sb("att_col", [P, 2], F32)
        head_rows = sb("head_rows", [P, H], F32)
        att_diag = sb("att_diag", [P, 2, H], F32)
        bias_b = sb("bias_b", [P, F], F32)
        ident = sb("ident", [P, P], F32)
        s_col = sb("s_col", [P, NT, H], F32)
        d_col = sb("d_col", [P, NT, H], F32)
        d_tr = sb("d_tr", [P, 2, P], F32)
        d_tr_first = sb("d_tr_first", [MB * H, P], F32)
        s_max1 = sb("s_max1", [P, H], F32)
        s_max = sb("s_max", [P, H], F32)
        s_neg = sb("s_neg", [P, NT, H], F32)
        s_steep = sb("s_steep", [P, NT, H], F32)
        s_shift = sb("s_shift", [P, NT, H], F32)
        d_shift = sb("d_shift", [P, NT, H], F32)
        p_exp = sb("p_exp", [P, NT, H], F32)
        q_exp = sb("q_exp", [P, NT, H], F32)
        ab_arg = sb("ab_arg", [P, NT, H, 2], F32)
        ab = sb("ab", [P, NT, H, 2], F32)
        den_inv = sb("den_inv", [P, MB * H, 1], F32)
        bn = sb("bn", [P, MB, 6], F32)
        mv = sb("mv", [P, MB, 2], F32)
        rstd = sb("rstd", [P, MB, 1], F32)
        shift = sb("shift", [P, MB, 1], F32)
        half = sb("half", [P, MB, 1], F32)
        warm = sb("warm", [P, 1], F32)
        minus_one = sb("minus_one", [P, MB, 1], F32)
        minus_lo = sb("minus_lo", [P, 1, 1], F32)

        params_loaded = sem("params_loaded")
        att_loaded = sem("att_loaded")
        att_ready = sem("att_ready")
        xt_loaded = [sem(f"xt_loaded{i}") for i in range(NXB)]
        ident_zeroed = sem("ident_zeroed")
        ident_ready = sem("ident_ready")
        bias_loaded = sem("bias_loaded")
        att_proj = sem("att_proj")
        w_ext_ready = sem("w_ext_ready")
        projected = sem("projected")
        feat_copied = sem("feat_copied")
        scores_copied = sem("scores_copied")
        d_transposed = sem("d_transposed")
        d_tr_ready = sem("d_tr_ready")
        d_stored = sem("d_stored")
        first_transposed = sem("first_transposed")
        first_ready = sem("first_ready")
        first_stored = sem("first_stored")
        dve_step = sem("dve_step")
        max1_ready = sem("max1_ready")
        max_ready = sem("max_ready")
        exp_args = sem("exp_args")
        first_thresholds = sem("first_thresholds")
        exps_ready = sem("exps_ready")
        exps_scaled = sem("exps_scaled")
        p_products = sem("p_products")
        q_products = sem("q_products")
        p_his = sem("p_his")
        q_his = sem("q_his")
        p_los = sem("p_los")
        q_los = sem("q_los")
        hi_scaled = sem("hi_scaled")
        vals_ready = sem("vals_ready")
        drow_loaded = [sem(f"drow_loaded{i}") for i in range(2)]
        xres_loaded = [sem(f"xres_loaded{i}") for i in range(2)]
        adj_loaded = [sem(f"adj_loaded{i}") for i in range(AU)]
        slot_free = sem("slot_free")
        act_masks = sem("act_masks")
        dve_masks = sem("dve_masks")
        masks_ready = sem("masks_ready")
        block_done = sem("block_done")
        block_free = sem("block_free")
        pool_step = sem("pool_step")
        comb_ready = sem("comb_ready")
        den_ready = sem("den_ready")
        den_inverted = sem("den_inverted")
        y_ready = sem("y_ready")
        rstd_ready = sem("rstd_ready")
        shift_ready = sem("shift_ready")
        bn_done = sem("bn_done")
        mv_ready = sem("mv_ready")
        out_ready = sem("out_ready")
        out_stored = sem("out_stored")

        xT_b = xT.rearrange("f (b n) -> b f n", b=NXB)
        adj_u = adj.rearrange("(u t p) m -> u p t m", u=UPC, t=UNIT * G)
        x_c = x.rearrange("(c j p) f -> c p j f", c=NCH, j=MB)
        out_c = out.rearrange("(c j p) f -> c p j f", c=NCH, j=MB)
        drow_c = scratch.rearrange("(c j) h p -> c (j h p)", c=NCH)

        def half_of(tmp, q):
            return tmp[:, q % 2 * QT * H * W:(q % 2 + 1) * QT * H * W]

        def part_views(q):
            tiles = slice(q * QT, (q + 1) * QT)
            return (vals_am[:, tiles].rearrange("p t h w -> p (t h) w"),
                    vals_a[:, tiles].rearrange("p t h w -> p (t h) w"),
                    half_of(stage_raw, q).rearrange("p (x w) -> p x w", w=W),
                    half_of(q_tmp, q).rearrange("p (x w) -> p x w", w=W))

        def times_head_factor(engine, tmp, h, e, tiles, done):
            ev = e[:, tiles].rearrange("p t h -> p (t h)").unsqueeze(2)
            tv = tmp.rearrange("p (x w) -> p x w", w=W)
            engine.tensor_tensor(tv[:, :, 0:FO], h[:, tiles].rearrange("p t h f -> p (t h) f"),
                                 ev.to_broadcast([P, QT * H, FO]), ALU.mult).then_inc(done, 1)
            engine.tensor_copy(tv[:, :, FO:W], ev).then_inc(done, 1)

        block = ctx.enter_context(nc.Block())

        @block.sync
        def _(sp):
            for k, att in enumerate((att_src, att_dst)):
                sp.dma_start(att_col[:, k:k + 1], att.rearrange("a h f -> (h f) a")).then_inc(att_loaded, 16)
            sp.dma_start(w_nat[:], weight).then_inc(params_loaded, 16)
            sp.dma_start(w_ext[:, 0:F], weightT).then_inc(params_loaded, 16)

            def load_xt(batches):
                for b in batches:
                    sp.dma_start(xt_sb[:, b * XB * P:(b + 1) * XB * P], xT_b[b]).then_inc(xt_loaded[b], 16)

            load_xt(range(NXB - 2))
            sp.wait_ge(first_ready, 1)
            sp.dma_start(first_scores, d_tr_first[:]).then_inc(first_stored, 16)
            load_xt(range(NXB - 2, NXB))
            sp.wait_ge(first_stored, 16)
            sp.dma_start(drow[:, 0].rearrange("p j h m -> p (j h m)"),
                         first_scores.rearrange("(a j) m -> a (j m)", a=1).to_broadcast([P, MB * H * P])).then_inc(
                             drow_loaded[0], 16)
            sp.dma_start(bias_b[:], bias.rearrange("(a f) -> a f", a=1).to_broadcast([P, F])).then_inc(
                bias_loaded, 16)
            sp.wait_ge(d_tr_ready, 1)
            sp.dma_start(scratch.rearrange("(k t) h p -> (t h) k p", k=2), d_tr[:]).then_inc(d_stored, 16)
            sp.wait_ge(d_stored, 16)

            def load_scores(c, k):
                sp.dma_start(drow[:, k].rearrange("p j h m -> p (j h m)"),
                             drow_c[bass.ds(c, 1), :].to_broadcast([P, MB * H * P])).then_inc(drow_loaded[k], 16)

            def load_x(c, k):
                sp.dma_start(x_res[:, k], x_c[bass.ds(c, 1)].rearrange("a p j f -> p (a j) f")).then_inc(
                    xres_loaded[k], 16)

            def store_chunk(c):
                sp.wait_ge(out_ready, c + 1)
                sp.dma_start(out_c[bass.ds(c, 1)].rearrange("a p j f -> p (a j) f"), y_out).then_inc(
                    out_stored, 16)

            load_scores(1, 1)
            for k in range(2):
                load_x(k, k)
            with sp.Fori(0, NCH // 2 - 1) as i:
                for k in range(2):
                    sp.wait_ge(act_masks, NG * (2 * i + k + 1))
                    sp.wait_ge(dve_masks, NG * (2 * i + k + 1))
                    load_scores(2 * i + k + 2, k)
                    store_chunk(2 * i + k)
                    load_x(2 * i + k + 2, k)
            store_chunk(NCH - 2)
            store_chunk(NCH - 1)
            sp.wait_ge(out_stored, 16 * NCH)

        @block.gpsimd
        def _(pool):
            nc.gpsimd.memset(ident[:], 0.0).then_inc(ident_zeroed, 1)
            pool.wait_ge(ident_zeroed, 1)
            nc.gpsimd.affine_select(out=ident[:], in_=ident[:], compare_op=ALU.not_equal, fill=1.0, base=0,
                                    pattern=[[-1, P]], channel_multiplier=1).then_inc(ident_ready, 1)
            nc.gpsimd.memset(minus_one[:], -1.0)
            nc.gpsimd.memset(minus_lo[:], -LO)
            nc.gpsimd.memset(half[:], -0.5).then_inc(pool_step, 1)
            pool.wait_ge(pool_step, 1)

            def load_adj(u):
                if u >= AU:
                    pool.wait_ge(slot_free, RING + UNIT * (u - AU + 1))
                pool.dma_start(adj8[:, u % AU].rearrange("p u t m -> p (u t) m"),
                               adj_u[u % UPC][:, :, (u // UPC) * MC:(u // UPC + 1) * MC]).then_inc(
                                   adj_loaded[u % AU], 16)

            STEPS = 5

            def combine(c):
                pool.wait_ge(comb_ready, c + 1)
                abv = ab[:, c * MB:(c + 1) * MB].rearrange("p j h s -> p (j h s)").unsqueeze(2)
                nc.gpsimd.tensor_tensor(comb, comb, abv.to_broadcast([P, 2 * MB * H, W]), ALU.mult).then_inc(
                    pool_step, 1)
                pool.wait_ge(pool_step, 2 + STEPS * c)

            def total(c):
                c2 = comb.rearrange("p (x s) w -> p x s w", s=2)
                nc.gpsimd.tensor_tensor(tot, c2[:, :, 0], c2[:, :, 1], ALU.add).then_inc(den_ready, 1)

            def residual(c):
                n = 2 + STEPS * c
                k = c % 2
                pool.wait_ge(xres_loaded[k], 16 * (c // 2 + 1))
                xv = x_res[:, k]
                nc.gpsimd.tensor_tensor(xv, xv, bias_b[:].unsqueeze(1).to_broadcast([P, MB, F]), ALU.add).then_inc(
                    pool_step, 1)
                pool.wait_ge(den_inverted, c + 1)
                if c:
                    pool.wait_ge(out_ready, c)
                yv = y.rearrange("p j (h f) -> p (j h) f", h=H)
                nc.gpsimd.tensor_tensor(yv, tot[:, :, 0:FO], den_inv[:].to_broadcast([P, MB * H, FO]),
                                        ALU.mult).then_inc(pool_step, 1)
                pool.wait_ge(pool_step, n + 2)
                nc.gpsimd.tensor_tensor(y, y, xv, ALU.add).then_inc(y_ready, 1)

            def inverse_std(c, n):
                pool.wait_ge(mv_ready, c + 1)
                nc.gpsimd.tensor_scalar(rstd[:], mv[:, :, 1:2], EPS, None, ALU.add).then_inc(pool_step, 1)
                pool.wait_ge(pool_step, n + 1)
                nc.gpsimd.tensor_tensor(rstd[:], rstd[:], half[:], ALU.pow).then_inc(rstd_ready, 1)

            def normaliser(c):
                n = 4 + STEPS * c
                inverse_std(c, n)
                pool.wait_ge(rstd_ready, c + 1)
                nc.gpsimd.tensor_tensor(shift[:], mv[:, :, 0:1], rstd[:], ALU.mult).then_inc(pool_step, 1)
                pool.wait_ge(pool_step, n + 2)
                nc.gpsimd.tensor_tensor(shift[:], shift[:], minus_one[:], ALU.mult).then_inc(shift_ready, 1)

            def chunk(c):
                for u in range(UPC):
                    if c:
                        load_adj(c * UPC + u)
                    if c and u == 3:
                        combine(c - 1)
                        total(c - 1)
                    if c and u == 4:
                        residual(c - 1)
                    if c and u == 6:
                        normaliser(c - 1)

            pool.wait_ge(xt_loaded[NXB - 1], 16)
            for u in range(AU):
                load_adj(u)
            pool.wait_ge(max1_ready, 1)
            nc.gpsimd.partition_all_reduce(s_max[:], s_max1[:], P, bass.bass_isa.ReduceOp.max).then_inc(
                max_ready, 1)

            def products(q):
                if q >= 2:
                    for read in (p_his, q_his, p_los, q_los):
                        pool.wait_ge(read, q - 1)
                tiles = slice(q * QT, (q + 1) * QT)
                if q >= 1:
                    pool.wait_ge(p_products, 2 * q)
                    times_head_factor(nc.gpsimd, half_of(stage_raw, q), feat, p_exp, tiles, p_products)
                times_head_factor(nc.gpsimd, half_of(q_tmp, q), feat, q_exp, tiles, q_products)

            def q_low(q):
                _, vq, _, qt = part_views(q)
                pool.wait_ge(q_los, q)
                pool.wait_ge(q_his, q + 1)
                nc.gpsimd.tensor_tensor(hi_tmp, vq[:, :, 0:W], minus_lo[:].to_broadcast([P, QT * H, W]),
                                        ALU.mult).then_inc(hi_scaled, 1)
                pool.wait_ge(hi_scaled, q)
                pool.wait_ge(q_products, 2 * (q + 1))
                nc.gpsimd.tensor_tensor(vq[:, :, W:2 * W], hi_tmp, qt, ALU.add).then_inc(q_los, 1)

            pool.wait_ge(exps_scaled, 1)
            for q in range(NQ + 1):
                if q < NQ:
                    products(q)
                if AU <= q < NQ:
                    load_adj(q)
                if q >= 2:
                    q_low(q - 1)
            pool.wait_ge(q_los, NQ)
            pool.wait_ge(bias_loaded, 16)
            for c in range(NCH):
                chunk(c)
            inverse_std(NCH - 1, 1 + STEPS * (NCH - 1))

        @block.scalar
        def _(act):
            def copy_features(batches):
                for b in batches:
                    act.wait_ge(projected, b + 1)
                    src = psum[:, MB * (b % 2):MB * (b % 2 + 1), 0:2 * (F + 2 * H)].rearrange(
                        "p a (t f) -> p a t f", t=2)[:, :, :, 0:F]
                    dst = feat[:, b * XB:(b + 1) * XB].rearrange("p (a t) h f -> p a t (h f)", t=2)
                    nc.scalar.activation(dst, src, ACT.Copy).then_inc(feat_copied, 1)

            def exponentials():
                act.wait_ge(exp_args, 1)
                nc.scalar.activation(p_exp[:], s_shift[:], ACT.Exp)
                nc.scalar.activation(q_exp[:], s_shift[:], ACT.Exp, scale=SLOPE)
                nc.scalar.activation(ab[:], ab_arg[:], ACT.Exp).then_inc(exps_ready, 1)

            def high_parts(q):
                va, vq, pt, qt = part_views(q)
                act.wait_ge(p_products, 2 * (q + 1))
                act.wait_ge(q_products, 2 * (q + 1))
                nc.scalar.activation(va[:, :, 0:W], pt, ACT.Copy, scale=1.0 / LO).then_inc(p_his, 1)
                nc.scalar.activation(vq[:, :, 0:W], qt, ACT.Copy, scale=1.0 / LO).then_inc(q_his, 1)

            def compare(c, k, g, extra=EXTRA):
                act.wait_ge(slot_free, NG * c + g + 1)
                act.sem_inc(passed["act"], 1)
                heads = [(h, t) for h in range(SPLIT) for t in range(G)] + [(SPLIT, 0)] * (g in extra)
                for h, t in heads:
                    n = g * G + t
                    last = nc.scalar.activation(
                        masks[:, g % RING, h, t, :].rearrange("p (j m) -> p j m", j=MB), drow[:, k, :, h, :],
                        ACT.Sigmoid, scale=STEEP, bias=s_steep[:, n, h:h + 1], saturate=False)
                last.then_inc(act_masks, 1)

            def copy_out(c, first=False):
                for j in range(MB):
                    if j < MB - 1:
                        act.wait_ge(block_done, (MB - 1) * c + j + 1)
                    else:
                        act.wait_ge(slot_free, RING + NG * (c + 1))
                    if j == 0 and not first:
                        act.wait_ge(comb_ready, c)
                    nc.scalar.activation(
                        stage_raw[:, j * H * VA:(j + 1) * H * VA].rearrange("p (a w) -> p a w", a=2),
                        psum[:, 2 * j:2 * j + 2, 0:2 * VA], ACT.Copy).then_inc(block_free, 1)

            def normalise(c, stores=True):
                act.wait_ge(shift_ready, c + 1)
                if stores:
                    act.wait_ge(out_stored, 16 * c)
                for j in range(MB):
                    last = nc.scalar.activation(y_out[:, j], y[:, j], ACT.Identity, scale=rstd[:, j],
                                                bias=shift[:, j])
                last.then_inc(out_ready, 1)

            def chunk(c, k, loads, stores=True):
                act.wait_ge(drow_loaded[k], 16 * loads)
                for g in range(NG):
                    compare(c, k, g)
                    if g == (2 if stores else 1):
                        copy_out(c - 1, first=not stores)
                    if g == 14:
                        normalise(c - 1, stores)

            copy_features(range(NXB))
            exponentials()
            nc.scalar.activation(warm[:], s_shift[:, 0, 0:1], ACT.Sigmoid)
            high_parts(0)
            act.sem_inc(act_masks, 1)
            act.wait_ge(drow_loaded[0], 16)
            for g in range(1, NG):
                compare(0, 0, g, EXTRA_FIRST)
                if g % GPQ == 1 and g + 1 < NG:
                    high_parts(g // GPQ + 1)
            chunk(1, 1, 1, stores=False)
            with act.Fori(1, NCH // 2) as i:
                chunk(2 * i, 0, i + 1)
                chunk(2 * i + 1, 1, i + 1)
            copy_out(NCH - 1)

        @block.vector
        def _(dve):
            steps = [0]

            def link(ins):
                steps[0] += 1
                ins.then_inc(dve_step, 1)
                dve.wait_ge(dve_step, steps[0])

            link(nc.vector.memset(head_rows[:], 0.0))
            for h in range(H):
                link(nc.vector.memset(head_rows[h * FO:(h + 1) * FO, h:h + 1], 1.0))
            dve.wait_ge(att_loaded, 32)
            nc.vector.tensor_tensor(att_diag[:], att_col[:].unsqueeze(2).to_broadcast([P, 2, H]),
                                    head_rows[:].unsqueeze(1).to_broadcast([P, 2, H]), ALU.mult).then_inc(
                                        att_ready, 1)
            dve.wait_ge(params_loaded, 32)
            dve.wait_ge(att_proj, 1)
            nc.vector.tensor_copy(w_ext[:, F:F + 2 * H], psum[:, 6, 0:2 * H]).then_inc(w_ext_ready, 1)

            def first_group_masks(h):
                dve.wait_ge(drow_loaded[0], 16)
                dve.wait_ge(first_thresholds, 1)
                for t in range(G):
                    last = nc.vector.tensor_scalar(
                        masks[:, 0, h, t, :].rearrange("p (j m) -> p j m", j=MB), drow[:, 0, :, h, :],
                        s_neg[:, t, h:h + 1], None, ALU.is_gt, saturate=False)
                if h == H - 1:
                    last.then_inc(dve_masks, 1)

            EARLY = NXB - H
            for b in range(NXB):
                dve.wait_ge(feat_copied, b + 1)
                src = psum[:, MB * (b % 2):MB * (b % 2 + 1), 0:2 * (F + 2 * H)].rearrange(
                    "p a (t f) -> p a t f", t=2)
                for k, col in enumerate((s_col, d_col)):
                    dst = col[:, b * XB:(b + 1) * XB].rearrange("p (a t) h -> p a t h", t=2)
                    last = nc.vector.tensor_copy(dst, src[:, :, :, F + k * H:F + (k + 1) * H])
                last.then_inc(scores_copied, 1)
                if b == 0:
                    dve.wait_ge(scores_copied, 1)
                    nc.vector.tensor_scalar(s_neg[:, 0:G], s_col[:, 0:G], -1.0, None, ALU.mult).then_inc(
                        first_thresholds, 1)
                    dve.wait_ge(first_transposed, 1)
                    nc.vector.tensor_copy(d_tr_first[:], psum[0:MB * H, 0, 0:P]).then_inc(first_ready, 1)
                if EARLY <= b < EARLY + H - 1:
                    first_group_masks(b - EARLY)
            dve.wait_ge(scores_copied, NXB)
            nc.vector.tensor_reduce(s_max1[:], s_col[:].rearrange("p t h -> p h t"), AX_X, ALU.max).then_inc(
                max1_ready, 1)
            nc.vector.tensor_scalar(s_neg[:, G:NT], s_col[:, G:NT], -1.0, None, ALU.mult)
            link(nc.vector.tensor_scalar(s_steep[:], s_col[:], STEEP, None, ALU.mult))
            dve.wait_ge(d_transposed, 1)
            nc.vector.tensor_copy(d_tr[:], psum[:, 0, 0:2 * P].rearrange("p (k m) -> p k m", k=2)).then_inc(
                d_tr_ready, 1)
            dve.wait_ge(max_ready, 1)
            sm = s_max[:].unsqueeze(1).to_broadcast([P, NT, H])
            nc.vector.tensor_tensor(s_shift[:], s_col[:], sm, ALU.subtract)
            link(nc.vector.tensor_tensor(d_shift[:], d_col[:], sm, ALU.add))
            nc.vector.tensor_scalar(ab_arg[:, :, :, 0], d_shift[:], 1.0 - SLOPE, 0.0, ALU.mult, ALU.min)
            nc.vector.tensor_scalar(ab_arg[:, :, :, 1], d_shift[:], SLOPE - 1.0, 0.0, ALU.mult, ALU.min).then_inc(
                exp_args, 1)
            first_group_masks(H - 1)
            dve.wait_ge(exps_ready, 1)
            nc.vector.tensor_scalar(q_exp[:], q_exp[:], HI_SCALE * LO, None, ALU.mult).then_inc(exps_scaled, 1)
            link(nc.vector.tensor_scalar(p_exp[:], p_exp[:], HI_SCALE * LO, None, ALU.mult))

            def low_parts(q):
                va, vq, pt, qt = part_views(q)
                work = [(pt, va, p_products, p_his, p_los)] + [(qt, vq, q_products, q_his, q_los)] * (q == 0)
                for tmp, v, made, his, los in work:
                    dve.wait_ge(made, 2 * (q + 1))
                    dve.wait_ge(his, q + 1)
                    nc.vector.scalar_tensor_tensor(out=v[:, :, W:2 * W], in0=v[:, :, 0:W], scalar=-LO, in1=tmp,
                                                   op0=ALU.mult, op1=ALU.add).then_inc(los, 1)

            def minus_q(q):
                va, vq, _, _ = part_views(q)
                dve.wait_ge(p_los, q + 1)
                dve.wait_ge(q_los, q + 1)
                nc.vector.tensor_scalar(va[:, :, VQ:VA], vq, -1.0, None, ALU.mult).then_inc(vals_ready, 1)

            def masks_of(c, k, g, extra=EXTRA):
                r = g % RING
                dve.wait_ge(slot_free, NG * c + g + 1)
                dve.sem_inc(passed["dve"], 1)
                for h in range(SPLIT, H):
                    for t in range(int(h == SPLIT and g in extra), G):
                        n = g * G + t
                        last = nc.vector.tensor_scalar(
                            masks[:, r, h, t, :].rearrange("p (j m) -> p j m", j=MB), drow[:, k, :, h, :],
                            s_neg[:, n, h:h + 1], None, ALU.is_gt, saturate=False)
                last.then_inc(dve_masks, 1)

            def and_adj(c, g):
                r = g % RING
                u = g // UNIT
                dve.wait_ge(adj_loaded[u % AU], 16 * ((UPC // AU) * c + u // AU + 1))
                for lo, hi, done in ((0, SPLIT, act_masks), (SPLIT, H, dve_masks)):
                    dve.wait_ge(done, NG * c + g + 1)
                    m = masks16[:, r, lo:hi]
                    a = adj16[:, u % AU, g % UNIT].unsqueeze(1).to_broadcast([P, hi - lo, G * MC // 2])
                    nc.vector.tensor_tensor(m, m, a, ALU.bitwise_and).then_inc(masks_ready, 1)

            def add_parts(c, first=False):
                dve.wait_ge(block_free, MB * (c + 2))
                if first:
                    dve.wait_ge(q_his, NQ)
                    dve.wait_ge(q_los, NQ)
                else:
                    dve.wait_ge(den_ready, c)
                nc.vector.scalar_tensor_tensor(out=comb, in0=sums[:, :, 1], scalar=1.0 / LO, in1=sums[:, :, 0],
                                               op0=ALU.mult, op1=ALU.add).then_inc(comb_ready, 1)

            def invert(c):
                dve.wait_ge(den_ready, c + 1)
                nc.vector.reciprocal(den_inv[:], tot[:, :, FO:W]).then_inc(den_inverted, 1)

            def stats(c):
                dve.wait_ge(y_ready, c + 1)
                for j in range(MB):
                    last = nc.vector.bn_stats(bn[:, j], y[:, j])
                last.then_inc(bn_done, 1)
                dve.wait_ge(bn_done, c + 1)
                dve.sem_inc(passed["dve"], 1)
                for j in range(MB):
                    last = nc.vector.bn_aggr(mv[:, j], bn[:, j])
                last.then_inc(mv_ready, 1)

            def chunk(c, k, loads, first=False):
                dve.wait_ge(drow_loaded[k], 16 * loads)
                for g in range(NG):
                    masks_of(c, k, g)
                    and_adj(c, g)
                    if g == 5:
                        add_parts(c - 1, first)
                    if g == 7:
                        invert(c - 1)
                    if g == 9:
                        stats(c - 1)

            times_head_factor(nc.vector, half_of(stage_raw, 0), feat, p_exp, slice(0, QT), p_products)
            and_adj(0, 0)
            low_parts(0)
            minus_q(0)
            for g in range(1, NG):
                masks_of(0, 0, g, EXTRA_FIRST)
                if g % GPQ == 0:
                    low_parts(g // GPQ)
                    minus_q(g // GPQ)
                and_adj(0, g)
            chunk(1, 1, 1, first=True)
            with dve.Fori(1, NCH // 2) as i:
                chunk(2 * i, 0, i + 1)
                chunk(2 * i + 1, 1, i + 1)

            e = NCH - 1
            PAIR = 2
            cj = comb[:, 0:PAIR * 2 * H]
            sums_of = sums.rearrange("p (j x) k w -> p j x k w", j=MB)
            c2 = cj.rearrange("p (x s) w -> p x s w", s=2)
            tj = tot[:, 0:PAIR * H]
            dve.wait_ge(xres_loaded[e % 2], 16 * NCH // 2)
            dve.wait_ge(y_ready, e)
            dve.wait_ge(out_stored, 16 * e)
            link(nc.vector.tensor_tensor(x_res[:, e % 2], x_res[:, e % 2],
                                         bias_b[:].unsqueeze(1).to_broadcast([P, MB, F]), ALU.add))
            for j in range(0, MB, PAIR):
                js = slice(j, j + PAIR)
                dve.wait_ge(block_free, MB * NCH + j + PAIR)
                part = sums_of[:, js].rearrange("p j x k w -> p (j x) k w")
                link(nc.vector.scalar_tensor_tensor(out=cj, in0=part[:, :, 1], scalar=1.0 / LO, in1=part[:, :, 0],
                                                    op0=ALU.mult, op1=ALU.add))
                abj = ab[:, MB * e + j:MB * e + j + PAIR].rearrange("p j h s -> p (j h s)").unsqueeze(2)
                link(nc.vector.tensor_tensor(cj, cj, abj.to_broadcast([P, PAIR * 2 * H, W]), ALU.mult))
                link(nc.vector.tensor_tensor(tj, c2[:, :, 0], c2[:, :, 1], ALU.add))
                link(nc.vector.reciprocal(den_inv[:, 0:PAIR * H], tj[:, :, FO:W]))
                link(nc.vector.tensor_tensor(y[:, js].rearrange("p j (h f) -> p (j h) f", h=H), tj[:, :, 0:FO],
                                             den_inv[:, 0:PAIR * H].to_broadcast([P, PAIR * H, FO]), ALU.mult))
                link(nc.vector.tensor_tensor(y[:, js], y[:, js], x_res[:, e % 2, js], ALU.add))
                for i in range(j, j + PAIR):
                    last = nc.vector.bn_stats(bn[:, i], y[:, i])
                link(last)
                for i in range(j, j + PAIR):
                    last = nc.vector.bn_aggr(mv[:, i], bn[:, i])
            last.then_inc(mv_ready, 1)
            dve.wait_ge(mv_ready, NCH)
            dve.wait_ge(rstd_ready, NCH)
            for j in range(MB):
                last = nc.vector.tensor_scalar(y_out[:, j], y[:, j], mv[:, j, 0:1], rstd[:, j],
                                               ALU.subtract, ALU.mult)
            last.then_inc(out_ready, 1)

        @block.tensor
        def _(pe):
            pe.sem_inc(slot_free, RING)
            pe.wait_ge(params_loaded, 32)
            pe.wait_ge(att_ready, 1)
            nc.tensor.matmul(psum[:, 6, 0:2 * H], w_nat[:], att_diag[:].rearrange("p k h -> p (k h)"),
                             start=True, stop=True).then_inc(att_proj, 1)
            pe.wait_ge(w_ext_ready, 1)
            for b in range(NXB):
                pe.wait_ge(xt_loaded[b], 16)
                if b == 2:
                    pe.wait_ge(ident_ready, 1)
                    pe.wait_ge(feat_copied, 1)
                    pe.wait_ge(scores_copied, 1)
                    nc.tensor.matmul(psum[0:MB * H, 0, 0:P], d_col[:, 0:MB].rearrange("p t h -> p (t h)"),
                                     ident[:], start=True, stop=True, skip_group_check=True).then_inc(
                                         first_transposed, 1)
                    pe.wait_ge(first_ready, 1)
                if b >= 2:
                    pe.wait_ge(feat_copied, b - 1)
                    pe.wait_ge(scores_copied, b - 1)
                for i in range(XB):
                    n = b * XB + i
                    o = (i % 2) * (F + 2 * H)
                    last = nc.tensor.matmul(psum[:, MB * (b % 2) + i // 2, o:o + F + 2 * H],
                                            xt_sb[:, n * P:(n + 1) * P], w_ext[:], start=True, stop=True,
                                            skip_group_check=True)
                last.then_inc(projected, 1)
            pe.wait_ge(ident_ready, 1)
            pe.wait_ge(scores_copied, NXB)
            for k in range(2):
                last = nc.tensor.matmul(psum[:, 0, k * P:(k + 1) * P],
                                        d_col[:, k * NT // 2:(k + 1) * NT // 2].rearrange("p t h -> p (t h)"),
                                        ident[:], start=True, stop=True, skip_group_check=True)
            last.then_inc(d_transposed, 1)
            pe.wait_ge(d_tr_ready, 1)
            pe.sem_inc(block_free, MB)

            with pe.Fori(0, NCH) as c:
                for g in range(NG):
                    r = g % RING
                    pe.wait_ge(masks_ready, 2 * (NG * c + g + 1))
                    pe.sem_inc(passed["pe"], 1)
                    if g % GPQ == 0:
                        pe.wait_ge(vals_ready, g // GPQ + 1)
                    for j in range(MB):
                        if g == 0:
                            pe.wait_ge(block_free, MB * c + j + 1)
                            pe.sem_inc(passed["pe"], 1)
                        js = slice(j * P, (j + 1) * P)
                        for t in range(G):
                            n = g * G + t
                            first, final = n == 0, n == NT - 1
                            for h in range(H):
                                o = (h % 2) * VA
                                nc.tensor.matmul(psum[:, 2 * j + h // 2, o:o + VA], masks[:, r, h, t, js],
                                                 vals_am[:, n, h, :], start=first and h % 2 == 0, stop=False,
                                                 skip_group_check=True)
                            for a in range(2):
                                o = psum[:, 2 * j + a, 0:2 * VA].rearrange("p (h w) -> p h w", h=2)[:, :, VQ:VA]
                                last = nc.tensor.matmul(o, adj8[:, g // UNIT % AU, g % UNIT, t, js],
                                                        vals_a[:, n, 2 * a:2 * a + 2, :],
                                                        start=False, stop=final, skip_group_check=True)
                        if g == NG - 1 and j < MB - 1:
                            last.then_inc(block_done, 1)
                    last.then_inc(slot_free, 1)

    return nc


_INS = ['x', 'xT', 'adj', 'L0_gnn_weight', 'weightT', 'L0_gnn_att_src', 'L0_gnn_att_dst', 'L0_gnn_bias']


def kernel(**inputs):
    import numpy as _np
    import concourse.bacc as _bacc
    from concourse import mybir as _mybir
    from concourse.bass_utils import run_bass_kernel_spmd as _run

    laid = {k: _np.asarray(v) for k, v in inputs.items()}
    laid['xT'] = laid['x'].T
    laid['weightT'] = laid['L0_gnn_weight'].T
    nc = _bacc.Bacc("TRN2", target_bir_lowering=False, num_devices=1)
    arrays, args = {}, []
    for name in _INS:
        a = _np.ascontiguousarray(laid[name])
        arrays[f"in_{name}_dram"] = a
        args.append(nc.dram_tensor(f"in_{name}_dram", a.shape, _mybir.dt.from_np(a.dtype),
                                   kind="ExternalInput").ap())
    out = nc.dram_tensor("out_dram", laid['x'].shape, _mybir.dt.float32, kind="ExternalOutput").ap()
    gat_kernel(nc, *args, out)
    r = _run(nc, [arrays], core_ids=[0])
    return r.results[0]["out_dram"]
```
